# Optimizing a Trainium2 kernel written in Bass

```python
import numpy as np
import jax
import jax.numpy as jnp

def _softmax(x, axis=-1):
    return jax.nn.softmax(x, axis=axis)

def _gelu(x):
    return jax.nn.gelu(x, approximate=True)

def _silu(x):
    return jax.nn.silu(x)

def _sigmoid(x):
    return jax.nn.sigmoid(x)

def _layernorm(x, axis=-1, eps=1e-05):
    m = jnp.mean(x, axis=axis, keepdims=True)
    v = jnp.var(x, axis=axis, keepdims=True)
    return (x - m) / jnp.sqrt(v + eps)

def _scatter_add(tgt, idx, src, axis=0):
    return tgt.at[idx].add(src)

def _segment_sum(src, seg, n):
    return jax.ops.segment_sum(src, seg, n)
kernel_name = 'mk_adj_resnorm_d2_adj_r2_0dbd99'

def setup_inputs(seed: int=0):
    np.random.seed(seed)
    _w = jnp.asarray

    def _rec_inputs():
        import jax
        import jax.numpy as jnp
        _gk = jax.random.key(seed)
        x = -0.000125 + 0.9999 * jax.random.normal(jax.random.fold_in(_gk, 1), (128, 128, 128), jnp.float32)
        _w = (1.0 + jnp.arange(128, dtype=jnp.float32)) ** (-0.5)
        _w = _w / _w.mean()
        _pij = jnp.clip(0.0625 * _w[:, None] * _w[None, :], 0.0, 1.0)
        _a = jax.random.uniform(jax.random.fold_in(_gk, 2), (128, 128)) < _pij
        _a = jnp.logical_or(_a, jnp.swapaxes(_a, -1, -2))
        _a = jnp.logical_or(_a, jnp.eye(128, dtype=bool))
        _af = _a.astype(jnp.float32)
        _af = _af * jax.random.uniform(jax.random.fold_in(_gk, 3), (128, 128), jnp.float32, 0.05, 0.000488281)
        adj = _af
        return (x, adj)
    x, adj = _rec_inputs()

    def _L0_gnn_setup():
        import jax, jax.numpy as jnp
        import numpy as np
        B, T, D, H = (64, 1024, 128, 128)
        MAX_SKIP = 4

        def _lstm_last(Wih, Whh, bih, bhh, xs):
            N, _, Hd = xs.shape
            bias = bih + bhh

            def step(carry, x_t):
                h, c = carry
                g = x_t @ Wih.T + h @ Whh.T + bias
                i, f, gg, o = jnp.split(g, 4, axis=-1)
                c = jax.nn.sigmoid(f) * c + jax.nn.sigmoid(i) * jnp.tanh(gg)
                h = jax.nn.sigmoid(o) * jnp.tanh(c)
                return ((h, c), None)
            init = (jnp.zeros((N, Hd), xs.dtype), jnp.zeros((N, Hd), xs.dtype))
            (h_last, _), _ = jax.lax.scan(step, init, jnp.swapaxes(xs, 0, 1))
            return h_last
        key = jax.random.key(seed)
        ks = jax.random.split(key, 8)
        s = 0.05
        x = jax.random.normal(ks[0], (B, T, D), jnp.float32)
        adj = jax.random.uniform(ks[1], (T, T), jnp.float32) / T
        Wg0 = jax.random.normal(ks[2], (D, H), jnp.float32) * s
        bg0 = jnp.zeros((H,), jnp.float32)
        Wg1 = jax.random.normal(ks[3], (H, H), jnp.float32) * s
        bg1 = jnp.zeros((H,), jnp.float32)
        Wih = jax.random.normal(ks[4], (MAX_SKIP, 4 * H, H), jnp.float32) * s
        Whh = jax.random.normal(ks[5], (MAX_SKIP, 4 * H, H), jnp.float32) * s
        bih = jax.random.normal(ks[6], (MAX_SKIP, 4 * H), jnp.float32) * s
        bhh = jax.random.normal(ks[7], (MAX_SKIP, 4 * H), jnp.float32) * s
        return dict(x=x, adj=adj, Wg0=Wg0, bg0=bg0, Wg1=Wg1, bg1=bg1, Wih=Wih, Whh=Whh, bih=bih, bhh=bhh)
    _L0_gnn_all = _L0_gnn_setup()
    _L0_gnn_in = {k: v for k, v in _L0_gnn_all.items() if k in ('Wg0', 'bg0', 'Wg1', 'bg1', 'Wih', 'Whh', 'bih', 'bhh')}
    del _L0_gnn_all

    def _L1_gnn_setup():
        import jax, jax.numpy as jnp
        import numpy as np
        B, N, D, H = (4, 2048, 128, 128)
        key = jax.random.key(seed)
        ks = jax.random.split(key, 10)
        base_features = jax.random.normal(ks[0], (B, N, D), dtype=jnp.float32)
        pc = (jax.random.uniform(ks[1], (N, N)) < 8.0 / N).astype(jnp.float32)
        pc = pc * (1.0 - jnp.eye(N, dtype=jnp.float32))
        neighbor_mask = jnp.clip(pc + pc.T + jnp.eye(N, dtype=jnp.float32), 0.0, 1.0)
        s = 1.0 / np.sqrt(D)
        Wq = jax.random.normal(ks[2], (D, H), dtype=jnp.float32) * s
        Wk = jax.random.normal(ks[3], (D, H), dtype=jnp.float32) * s
        Wv = jax.random.normal(ks[4], (D, H), dtype=jnp.float32) * s
        Wo = jax.random.normal(ks[5], (H, D), dtype=jnp.float32) * (1.0 / np.sqrt(H))
        bq = jnp.zeros((H,), jnp.float32)
        bk = jnp.zeros((H,), jnp.float32)
        bv = jnp.zeros((H,), jnp.float32)
        bo = jnp.zeros((D,), jnp.float32)
        alpha = jnp.asarray(2.0, jnp.float32)
        gamma = jnp.asarray(0.3, jnp.float32)
        return dict(base_features=base_features, neighbor_mask=neighbor_mask, parent_child_mask=pc, Wq=Wq, bq=bq, Wk=Wk, bk=bk, Wv=Wv, bv=bv, Wo=Wo, bo=bo, alpha=alpha, gamma=gamma)
    _L1_gnn_all = _L1_gnn_setup()
    _L1_gnn_in = {k: v for k, v in _L1_gnn_all.items() if k in ('Wq', 'bq', 'Wk', 'bk', 'Wv', 'bv', 'Wo', 'bo', 'alpha', 'gamma')}
    del _L1_gnn_all
    return {'x': x, 'adj': adj, 'L0_gnn_Wg0': _L0_gnn_in['Wg0'], 'L0_gnn_bg0': _L0_gnn_in['bg0'], 'L0_gnn_Wg1': _L0_gnn_in['Wg1'], 'L0_gnn_bg1': _L0_gnn_in['bg1'], 'L0_gnn_Wih': _L0_gnn_in['Wih'], 'L0_gnn_Whh': _L0_gnn_in['Whh'], 'L0_gnn_bih': _L0_gnn_in['bih'], 'L0_gnn_bhh': _L0_gnn_in['bhh'], 'L1_gnn_Wq': _L1_gnn_in['Wq'], 'L1_gnn_bq': _L1_gnn_in['bq'], 'L1_gnn_Wk': _L1_gnn_in['Wk'], 'L1_gnn_bk': _L1_gnn_in['bk'], 'L1_gnn_Wv': _L1_gnn_in['Wv'], 'L1_gnn_bv': _L1_gnn_in['bv'], 'L1_gnn_Wo': _L1_gnn_in['Wo'], 'L1_gnn_bo': _L1_gnn_in['bo'], 'L1_gnn_alpha': _L1_gnn_in['alpha'], 'L1_gnn_gamma': _L1_gnn_in['gamma']}

def reference(x, adj, L0_gnn_Wg0, L0_gnn_bg0, L0_gnn_Wg1, L0_gnn_bg1, L0_gnn_Wih, L0_gnn_Whh, L0_gnn_bih, L0_gnn_bhh, L1_gnn_Wq, L1_gnn_bq, L1_gnn_Wk, L1_gnn_bk, L1_gnn_Wv, L1_gnn_bv, L1_gnn_Wo, L1_gnn_bo, L1_gnn_alpha, L1_gnn_gamma):
    import jax
    import jax.numpy as jnp

    def _L0_gnn_ref(x, adj, Wg0, bg0, Wg1, bg1, Wih, Whh, bih, bhh):
        import jax, jax.numpy as jnp
        import numpy as np
        B, T, D, H = (64, 1024, 128, 128)
        MAX_SKIP = 4

        def _lstm_last(Wih, Whh, bih, bhh, xs):
            N, _, Hd = xs.shape
            bias = bih + bhh

            def step(carry, x_t):
                h, c = carry
                g = x_t @ Wih.T + h @ Whh.T + bias
                i, f, gg, o = jnp.split(g, 4, axis=-1)
                c = jax.nn.sigmoid(f) * c + jax.nn.sigmoid(i) * jnp.tanh(gg)
                h = jax.nn.sigmoid(o) * jnp.tanh(c)
                return ((h, c), None)
            init = (jnp.zeros((N, Hd), xs.dtype), jnp.zeros((N, Hd), xs.dtype))
            (h_last, _), _ = jax.lax.scan(step, init, jnp.swapaxes(xs, 0, 1))
            return h_last
        h = jax.nn.relu(jnp.einsum('ts,bsh->bth', adj, x @ Wg0 + bg0))
        h = jax.nn.relu(jnp.einsum('ts,bsh->bth', adj, h @ Wg1 + bg1))
        Bv, Tv, Hd = h.shape
        for p in range(1, MAX_SKIP + 1):
            nw = Tv // p
            wins = h[:, :nw * p, :].reshape(Bv * nw, p, Hd)
            last = _lstm_last(Wih[p - 1], Whh[p - 1], bih[p - 1], bhh[p - 1], wins)
            idx = jnp.arange(nw) * p + (p - 1)
            h = h.at[:, idx, :].set(last.reshape(Bv, nw, Hd))
        return h

    def _L1_gnn_ref(base_features, neighbor_mask, parent_child_mask, Wq, bq, Wk, bk, Wv, bv, Wo, bo, alpha, gamma):
        import jax, jax.numpy as jnp
        import numpy as np
        B, N, D, H = (4, 2048, 128, 128)
        x = base_features
        Q = x @ Wq + bq
        K = x @ Wk + bk
        V = x @ Wv + bv
        scale = 1.0 / jnp.sqrt(jnp.asarray(K.shape[-1], x.dtype))
        scores = jnp.einsum('bnh,bmh->bnm', Q, K) * scale
        scores = scores + parent_child_mask[None] * alpha
        scores = jnp.where(neighbor_mask[None] == 0, jnp.asarray(-1000000000.0, x.dtype), scores)
        attn = jax.nn.softmax(scores, axis=-1)
        attn_out = jnp.einsum('bnm,bmh->bnh', attn, V)
        refined = attn_out @ Wo + bo + x
        child_sum = jnp.einsum('nm,bmd->bnd', parent_child_mask, refined)
        is_parent = (parent_child_mask.sum(axis=1) > 0).astype(x.dtype)
        delta = gamma * (child_sum - refined)
        return refined + delta * is_parent[None, :, None]
    x = _layernorm(x + _L0_gnn_ref(x, adj, L0_gnn_Wg0, L0_gnn_bg0, L0_gnn_Wg1, L0_gnn_bg1, L0_gnn_Wih, L0_gnn_Whh, L0_gnn_bih, L0_gnn_bhh), axis=-1)
    x = _layernorm(x + _L1_gnn_ref(x, adj, adj, L1_gnn_Wq, L1_gnn_bq, L1_gnn_Wk, L1_gnn_bk, L1_gnn_Wv, L1_gnn_bv, L1_gnn_Wo, L1_gnn_bo, L1_gnn_alpha, L1_gnn_gamma), axis=-1)
    return x

_drawn_inputs = setup_inputs


def setup_inputs(seed=0):
    import zlib

    import numpy as np

    out = dict(_drawn_inputs(seed))
    spreads = {'L0_gnn_bg0': (0.0, 0.8),
     'L0_gnn_bg1': (0.0, 0.8),
     'L1_gnn_bq': (0.0, 0.578),
     'L1_gnn_bk': (0.0, 0.8),
     'L1_gnn_bv': (0.0, 0.1),
     'L1_gnn_bo': (0.0, 0.1)}
    factors = {'L0_gnn_Wg0': 8.0,
     'L0_gnn_Wg1': 8.0,
     'L0_gnn_Wih': 6.582,
     'L0_gnn_Whh': 8.0,
     'L0_gnn_bhh': 2.686}
    for name, (base, spread) in spreads.items():
        noise = np.random.default_rng([zlib.crc32(name.encode()), seed]).standard_normal(out[name].shape)
        drawn = base * np.exp(spread * noise) if base else spread * noise
        out[name] = jnp.asarray(drawn.astype(out[name].dtype))
    for name, factor in factors.items():
        out[name] = (out[name] * factor).astype(out[name].dtype)
    return out
```

```python
from contextlib import ExitStack

import concourse.bass as bass
from concourse import mybir

F32 = mybir.dt.float32
F32R = mybir.dt.float32r
ALU = mybir.AluOpType
ACT = mybir.ActivationFunctionType
AX = mybir.AxisListType

NB, T, D = 128, 128, 128
GB, QB = 16, 4
NG, NQ = NB // GB, GB // QB
QW = QB * T
GW = GB * T
MAX_SKIP = 4
EPS = 1e-5
MASKED = -1e30
SCALE = float(D) ** -0.5


GI, GF, GG, GO = range(4)

STEPS = ([(1, c, 0) for c in range(4)]
         + [(2, c, s) for s in range(2) for c in range(2)]
         + [(3, c, s) for s in range(3) for c in range(2)]
         + [(4, 0, s) for s in range(4)])
NCHUNK = {1: 4, 2: 2, 3: 2, 4: 1}
NSTEP = len(STEPS)
NSPLIT = NSTEP - 1

GRAPH = ("AGG1", "PROJ1", "AGG2", "PROJ2")
ATTN = ("LN1", "XT", "KQ", "VAL", "ROW", "SCORE", "MIX", "OUT")
FILL = [
    [("LN1", 0), ("AGG1", 0)],
    [("LN1", 1)],
    [("LN1", 2), ("PROJ1", 0)],
    [("LN1", 3), ("XT", 0)],
    [("AGG2", 0), ("KQ", 0)],
    [("VAL", 0), ("ROW", 0), ("SCORE", 0)],
    [("XT", 1), ("PROJ2", 0)],
    [("KQ", 1), ("AGG1", 1), ("VAL", 1)],
    [("PROJ1", 1), ("ROW", 1), ("SCORE", 1)],
    [("MIX", 0), ("XT", 2), ("AGG2", 1)],
    [("OUT", 0), ("KQ", 2)],
    [("VAL", 2), ("PROJ2", 1)],
    [("MIX", 1), ("ROW", 2), ("SCORE", 2)],
    [("XT", 3), ("OUT", 1), ("AGG1", 2)],
    [("KQ", 3), ("VAL", 3), ("PROJ1", 2)],
    [("MIX", 2), ("AGG1", 3), ("ROW", 3), ("SCORE", 3), ("AGG2", 2)],
    [("OUT", 2), ("PROJ1", 3), ("PROJ2", 2)],
    [("AGG2", 3), ("MIX", 3), ("PROJ2", 3), ("OUT", 3)],
]
ORDER = [job for slot in FILL for job in slot]
FIRST = [sum(len(s) for s in FILL[:k]) for k in range(NSTEP + 1)]

ACT_PARTS = {"AGG1": [("hi", 0)], "PROJ1": [("hi", 1)], "AGG2": [("hi", 0)], "PROJ2": [("hi", 1)],
             "XT": [("hi", 0)], "KQ": [("hi", 0)], "VAL": [("hi", 0)],
             "SCORE": [("exp", 1), ("hi", 3)], "MIX": [("hi", 0)]}
DVE_PARTS = {"AGG1": [("lo", 1)], "PROJ1": [("sum", 0), ("lo", 2)], "AGG2": [("lo", 1)],
             "PROJ2": [("sum", 0), ("lo", 2)], "LN1": [("sum", 0)], "XT": [("lo", 1)],
             "KQ": [("lo", 1)], "VAL": [("lo", 1)], "ROW": [("copy", 0)],
             "SCORE": [("sum", 0), ("inv", 2), ("lo", 4)], "MIX": [("lo", 1)], "OUT": [("sum", 0)]}
POOL_PARTS = {"LN1": [("norm", 0)], "KQ": [("split", 0)], "SCORE": [("norm", 2)],
              "OUT": [("norm", 0)]}
SP_PARTS = {"KQ": [("load", 0)], "OUT": [("store", 0)]}


def due(parts, position):
    found = []
    for back in range(min(position, 4), -1, -1):
        at = position - back
        if at < len(ORDER):
            stage, q = ORDER[at]
            found += [(stage, q, part) for part, delay in parts.get(stage, []) if delay == back]
    return found


def graph_resnorm_kernel(nc, x, adj, Wg0, bg0, Wg1, bg1, Wih, Whh, bih, bhh,
                         Wq, bq, Wk, bk, Wv, bv, Wo, bo, alpha, gamma, out):
    with ExitStack() as ctx:
        def sb(name, cols, dt=F32, rows=128):
            return ctx.enter_context(nc.sbuf_tensor(name, [rows, cols], dt))

        def sem(name):
            return ctx.enter_context(nc.semaphore(name))

        def quad(ap):
            return ap.rearrange("p (b t) -> p b t", b=QB)

        def spread(ap):
            return ap.unsqueeze(1).to_broadcast([128, QB, 128])

        gate_bank = [ctx.enter_context(nc.psum_tensor(f"gate_bank{i}", [128, 512], F32)) for i in range(4)]
        side_bank = [ctx.enter_context(nc.psum_tensor(f"side_bank{i}", [128, 512], F32)) for i in range(4)]

        ident = sb("ident", 128)
        adjT = [sb(f"adjT_{h}", 128, F32R) for h in ("hi", "lo")]
        wg0 = [sb(f"wg0_{h}", 128, F32R) for h in ("hi", "lo")]
        wg1 = [sb(f"wg1_{h}", 128, F32R) for h in ("hi", "lo")]
        kq = [sb(f"kq_{h}", 128, F32R) for h in ("hi", "lo")]
        vo = [sb(f"vo_{h}", 128, F32R) for h in ("hi", "lo")]
        row = [sb(f"row_{h}", 2, F32R) for h in ("hi", "lo")]
        mixT = [sb(f"mixT_{h}", 128, F32R) for h in ("hi", "lo")]
        resT = [sb(f"resT_{h}", 128, F32R) for h in ("hi", "lo")]
        wih = [sb(f"wih_{h}", 16 * 128, F32R) for h in ("hi", "lo")]
        whh = [sb(f"whh_{h}", 12 * 128, F32R) for h in ("hi", "lo")]
        gate_bias = sb("gate_bias", 16)
        bias1 = sb("bias1", 128)
        bias2 = sb("bias2", 128)
        key_bias = sb("key_bias", 1)
        mask_bias = sb("mask_bias", 128)
        out_bias = sb("out_bias", 128)
        half = sb("half", 8)
        one = sb("one", 1)
        inv_d = sb("inv_d", 4)
        eps = sb("eps", 4)
        neg_half = sb("neg_half", 4)

        xg = sb("xg", GW)
        xs = [[sb(f"xs{n}_{h}", QW, F32R) for h in ("hi", "lo")] for n in range(2)]
        agg1 = [sb(f"agg1_{h}", QW, F32R) for h in ("hi", "lo")]
        sum1 = sb("sum1", QW)
        h1 = [sb(f"h1_{h}", QW, F32R) for h in ("hi", "lo")]
        agg2 = [sb(f"agg2_{h}", QW, F32R) for h in ("hi", "lo")]
        sum2 = sb("sum2", QW)
        h2 = [sb(f"h2_{h}", GW, F32R) for h in ("hi", "lo")]

        state = [sb(f"state_{h}", GW, F32R) for h in ("hi", "lo")]
        final = sb("final", GW)
        gates = sb("gates", 2 * 4 * 512)
        cell = sb("cell", 2 * 512)
        cell_tanh = sb("cell_tanh", 512)
        fresh = sb("fresh", 512)
        hidden = [[sb(f"hidden{n}_{h}", 512, F32R) for h in ("hi", "lo")] for n in range(2)]

        x1 = sb("x1", GW)
        stats1 = sb("stats1", 4 * 6)
        stats2 = sb("stats2", 4 * 6)
        moments = sb("moments", 8 * 4)
        x1s = [[sb(f"x1s{n}_{h}", QW, F32R) for h in ("hi", "lo")] for n in range(3)]
        x1T = [[sb(f"x1T{n}_{h}", QW, F32R) for h in ("hi", "lo")] for n in range(2)]
        query = [sb(f"query_{h}", QW, F32R) for h in ("hi", "lo")]
        value = [[sb(f"value{n}_{h}", QW, F32R) for h in ("hi", "lo")] for n in range(2)]
        row_shift = sb("row_shift", 2 * QB)
        score = sb("score", QW)
        neg_max = sb("neg_max", QB)
        expo = sb("expo", QW)
        exp_sum = sb("exp_sum", QB)
        exp_inv = sb("exp_inv", QB)
        prob = sb("prob", QW)
        probs = [sb(f"probs_{h}", QW, F32R) for h in ("hi", "lo")]
        mix = [sb(f"mix_{h}", QW, F32R) for h in ("hi", "lo")]
        y2 = [sb(f"y2_{n}", QW) for n in range(2)]

        const_loaded = sem("const_loaded")
        lstm_loaded = sem("lstm_loaded")
        setup_pe = sem("setup_pe")
        setup_act = sem("setup_act")
        setup_dve = sem("setup_dve")
        setup_pool = sem("setup_pool")
        xg_loaded = [sem(f"xg_loaded{q}") for q in range(NQ)]
        x1_loaded = [sem(f"x1_loaded{q}") for q in range(NQ)]
        y2_stored = [sem(f"y2_stored{n}") for n in range(2)]
        gate_ready = [sem(f"gate_ready{i}") for i in range(4)]
        gate_read = [sem(f"gate_read{i}") for i in range(4)]
        side_ready = [sem(f"side_ready{i}") for i in range(4)]
        side_read = [sem(f"side_read{i}") for i in range(4)]
        cell_term = sem("cell_term")
        cell_ready = sem("cell_ready")
        cell_tanh_ready = sem("cell_tanh_ready")
        h_full = sem("h_full")
        h_hi = sem("h_hi")
        h_split = sem("h_split")
        act_hi = {s: sem(f"hi_{s}") for s in ("AGG1", "PROJ1", "AGG2", "PROJ2", "XT", "KQ", "VAL", "SCORE", "MIX")}
        x_hi = sem("x_hi")
        x_split = sem("x_split")
        x1_hi = sem("x1_hi")
        pool_step = sem("pool_step")
        h1_split = sem("h1_split")
        h2_split = sem("h2_split")
        y1_ready = sem("y1_ready")
        y1_stats = sem("y1_stats")
        x1_ready = sem("x1_ready")
        x1_split = sem("x1_split")
        score_max = sem("score_max")
        exp_ready = sem("exp_ready")
        exp_inverse = sem("exp_inverse")
        prob_ready = sem("prob_ready")
        prob_split = sem("prob_split")
        y2_stats = sem("y2_stats")
        y2_ready = sem("y2_ready")

        def f32(ap):
            return ap.bitcast(F32)

        def wait(eng, s, value):
            if not isinstance(value, int) or value > 0:
                eng.wait_ge(s, value)

        def nth(group, q):
            return group * NQ + (q + 1)

        def bat(ap, b):
            return ap[:, b * 128:(b + 1) * 128]

        def has_graph(it):
            return not isinstance(it, int) or it + 1 < NG

        def has_lstm(it):
            return not isinstance(it, int) or 0 <= it < NG

        def has_attn(it):
            return not isinstance(it, int) or it >= 1

        def present(it, stage):
            return has_graph(it) if stage in GRAPH else has_attn(it)

        def jobs_before(it):
            graph_jobs, attn_jobs = len(GRAPH) * NQ // 4, len(ATTN) * NQ // 4
            if isinstance(it, int):
                return graph_jobs * min(it + 1, NG) + attn_jobs * max(it - 1, 0)
            return it * (graph_jobs + attn_jobs) + (graph_jobs - attn_jobs)

        def turn(it, stage, q):
            mine = [job for job in ORDER if present(it, job[0])].index((stage, q))
            return mine % 4, jobs_before(it) + mine // 4

        def products_done(eng, it, stage, q):
            bank, before = turn(it, stage, q)
            wait(eng, side_ready[bank], before + 1)

        def bank_read(eng, it, stage, q):
            bank, before = turn(it, stage, q)
            wait(eng, side_read[bank], before + 1)

        def gate_uses(it, gate, k):
            def uses(steps):
                return sum(1 for _, _, s in steps if gate != GF or s > 0)
            return it * uses(STEPS) + uses(STEPS[:k])

        def window(tile, p, chunk, s):
            nb = GB // NCHUNK[p]
            nw = T // p
            return tile[:, chunk * nb * T:(chunk + 1) * nb * T].rearrange(
                "h (b t) -> h b t", b=nb)[:, :, s:s + p * (nw - 1) + 1:p]

        def packed(tile, p):
            nb = GB // NCHUNK[p]
            nw = T // p
            return tile[:, 0:nb * nw].rearrange("h (b w) -> h b w", b=nb)

        def gate_tile(k, gate):
            at = ((k % 2) * 4 + gate) * 512
            return gates[:, at:at + 512]

        def w_index(p, gate):
            return (p - 1) * 4 + gate

        raw_ih = final
        raw_hh = x1
        raw = gates
        raw_at = {n: raw[:, i * 128:(i + 1) * 128] for i, n in enumerate(
            ("adj", "Wq", "Wk", "Wv", "Wo", "Wg0", "Wg1", "bg0", "bg1", "bo"))}
        transposed = raw[:, 1280:1792]
        adjT_f, wqT, wkT, wvT = (transposed[:, i * 128:(i + 1) * 128] for i in range(4))
        bq_wide = raw[:, 1792:1920]
        bv_wide = raw[:, 1920:2048]
        mixing = raw[:, 2048:2176]
        diagonal = raw[:, 2176:2304]
        mixT_f = raw[:, 2304:2432]
        resT_f = raw[:, 2432:2560]
        shift_rows = raw[:, 2560:2688]
        columns = raw[:, 2688:2704]
        bq_col, bk_col, bv_col, alpha_col, gamma_col = (columns[:, i:i + 1] for i in range(5))
        row_sum, parent, keep, row_const = (columns[:, i:i + 1] for i in range(5, 9))
        row_f = raw[:, 2704:2706]
        bih_rows = raw[0:16, 2816:2944]
        bhh_rows = raw[0:16, 2944:3072]

        N_CONST = 15
        (PE_TRANSPOSED, PE_FOLDED, PE_SHIFTS, PE_MIXT, PE_OUTBIAS) = range(1, 6)
        PE_BIAS = 6
        PE_LSTM = 7
        LSTM_JOBS = [("ih", 1), ("ih", 2), ("ih", 3), ("ih", 4), ("hh", 2), ("hh", 3), ("hh", 4)]
        GATE_PARTS = [(0, 2, 0.5), (2, 3, 1.0), (3, 4, 0.5)]
        DVE_TRANSPOSED, DVE_WIDE = 1, 3
        SETUP = {}

        def lstm_scale(kind, p, s):
            return s if kind == "ih" and p == 1 else 0.5 * s

        def lstm_dst(kind, p, half_index):
            w, base = (wih, (p - 1) * 4) if kind == "ih" else (whh, (p - 2) * 4)
            return w[half_index][:, base * 128:(base + 4) * 128]

        DVE_AP = 8
        DVE_MIXT = 9
        DVE_SHIFT_ROWS = 10
        DVE_BIAS_ROWS = 11
        SETUP_DVE = 39 + 3 * len(LSTM_JOBS)
        SETUP_ACT = 1 + 3 * len(LSTM_JOBS)

        block = ctx.enter_context(nc.Block())

        def iterations(eng, body):
            for it in (-1, 0, 1):
                body(it)
            with eng.Fori(2, NG - 1) as it:
                body(it)
            for it in (NG - 1, NG):
                body(it)

        x_quads = x.rearrange("(n b) t d -> n t b d", b=QB)
        out_quads = out.rearrange("(n b) t d -> n t b d", b=QB)

        @block.sync
        def _(sp):
            def load_const(dst, src):
                sp.dma_start(dst, src).then_inc(const_loaded, 16)

            with nc.allow_non_contiguous_dma(reason="bias columns, 4 bytes each"):
                load_const(raw_at["adj"], adj)
                for name, w in (("Wq", Wq), ("Wk", Wk), ("Wv", Wv), ("Wo", Wo), ("Wg0", Wg0), ("Wg1", Wg1)):
                    load_const(raw_at[name], w)
                for name, b in (("bg0", bg0), ("bg1", bg1), ("bo", bo)):
                    load_const(raw_at[name], b.rearrange("(a d) -> a d", a=1).to_broadcast([128, 128]))
                for col, b in ((bq_col, bq), (bk_col, bk), (bv_col, bv)):
                    load_const(col, b.rearrange("(d a) -> d a", a=1))
                for col, b in ((alpha_col, alpha), (gamma_col, gamma)):
                    load_const(col, b.rearrange("(a d) -> a d", a=1).to_broadcast([128, 1]))
                for q in range(NQ):
                    sp.dma_start(quad(xg[:, q * QW:(q + 1) * QW]), x_quads[q]).then_inc(xg_loaded[q], 16)
                sp.dma_start(raw_ih[:].rearrange("r (g h) -> r g h", g=16),
                             Wih.rearrange("p (g r) h -> r (p g) h", g=4)).then_inc(lstm_loaded, 16)
                sp.dma_start(raw_hh[:].rearrange("r (g h) -> r g h", g=16),
                             Whh.rearrange("p (g r) h -> r (p g) h", g=4)).then_inc(lstm_loaded, 16)
                sp.dma_start(bih_rows, bih.rearrange("p (g h) -> (p g) h", g=4)).then_inc(lstm_loaded, 16)
                sp.dma_start(bhh_rows, bhh.rearrange("p (g h) -> (p g) h", g=4)).then_inc(lstm_loaded, 16)

            def body(it):
                if has_graph(it) and (not isinstance(it, int) or it >= 0):
                    for q in range(NQ):
                        wait(sp, x_split, nth(it, q))
                        sp.dma_start(quad(xg[:, q * QW:(q + 1) * QW]),
                                     x_quads[(it + 1) * NQ + q]).then_inc(xg_loaded[q], 16)
                for stage, q in ORDER:
                    if stage == "KQ" and has_lstm(it):
                        if has_attn(it):
                            wait(sp, x1_split, nth(it - 1, q))
                        if isinstance(it, int) and it == 0:
                            sp.wait_ge(setup_dve, SETUP_DVE)
                        sp.dma_start(quad(x1[:, q * QW:(q + 1) * QW]),
                                     x_quads[it * NQ + q]).then_inc(x1_loaded[q], 16)
                    if stage == "OUT" and has_attn(it):
                        wait(sp, y2_ready, nth(it - 1, q))
                        sp.dma_start(out_quads[(it - 1) * NQ + q], quad(y2[q % 2][:])).then_inc(y2_stored[q % 2], 16)
            iterations(sp, body)
            for n in range(2):
                sp.wait_ge(y2_stored[n], 16 * NG * NQ // 2)

        @block.gpsimd
        def _(pool):
            pool.memset(half[:], 0.5).then_inc(setup_pool, 1)
            pool.memset(one[:], 1.0).then_inc(setup_pool, 1)
            pool.memset(inv_d[:], 1.0 / D).then_inc(setup_pool, 1)
            pool.memset(eps[:], EPS).then_inc(setup_pool, 1)
            pool.memset(neg_half[:], -0.5).then_inc(setup_pool, 1)
            pool.memset(ident[:], 0.0).then_inc(setup_pool, 1)
            pool.wait_ge(setup_pool, 6)
            pool.affine_select(out=ident[:], in_=ident[:], compare_op=ALU.not_equal, fill=1.0,
                               base=0, pattern=[[-1, 128]], channel_multiplier=1).then_inc(setup_pool, 1)

            chained = [0]

            def body(it):
                ln_per_it = 2 * 10 * NQ
                if isinstance(it, int):
                    base = ln_per_it * max(it - 1, 0)
                else:
                    base = ln_per_it * (it - 1)
                chained[0] = 0

                def step(ins):
                    chained[0] += 1
                    ins.then_inc(pool_step, 1)
                    pool.wait_ge(pool_step, base + chained[0])

                def normalise(stats, tile, ready):
                    st = stats[:].rearrange("p (b s) -> p b s", s=6)
                    m = moments[:].rearrange("p (k b) -> p k b", b=QB)
                    pair = moments[:, 0:8].rearrange("p (k b) -> p b k", b=QB)
                    tt = pool.tensor_tensor
                    step(tt(pair, st[:, :, 1:5:3], half[:].rearrange("p (b k) -> p b k", b=QB), ALU.mult))
                    step(tt(m[:, 2], m[:, 0], m[:, 1], ALU.add))
                    step(tt(m[:, 3], m[:, 0], m[:, 1], ALU.subtract))
                    step(tt(m[:, 4], st[:, :, 2], st[:, :, 5], ALU.add))
                    step(tt(m[:, 5], m[:, 4], inv_d[:], ALU.mult))
                    step(tt(m[:, 6], m[:, 3], m[:, 3], ALU.mult))
                    step(tt(m[:, 7], m[:, 5], m[:, 6], ALU.add))
                    step(tt(m[:, 5], m[:, 7], eps[:], ALU.add))
                    step(tt(m[:, 6], m[:, 5], neg_half[:], ALU.pow))
                    step(tt(quad(tile), quad(tile), m[:, 2].unsqueeze(2).to_broadcast([128, QB, 128]), ALU.subtract))
                    tt(quad(tile), quad(tile), m[:, 6].unsqueeze(2).to_broadcast([128, QB, 128]),
                       ALU.mult).then_inc(ready, 1)

                def split_x(q):
                    g = it + 1
                    n = q % 2
                    src = xg[:, q * QW:(q + 1) * QW]
                    wait(pool, xg_loaded[q], 16 * (g + 1))
                    if not isinstance(it, int) or it >= 0 or q >= 2:
                        if q >= 2:
                            bank_read(pool, it, "AGG1", q - 2)
                        elif has_graph(it - 1):
                            bank_read(pool, it - 1, "AGG1", q + 2)
                    pool.tensor_tensor(xs[n][0][:], src, one[:].to_broadcast([128, QW]), ALU.mult).then_inc(x_hi, 1)
                    wait(pool, x_hi, nth(g, q))
                    pool.tensor_tensor(xs[n][1][:], src, f32(xs[n][0][:]), ALU.subtract).then_inc(x_split, 1)

                if has_graph(it):
                    split_x(0)
                    split_x(1)
                for k in range(NSTEP):
                    for position in range(FIRST[k], FIRST[k + 1] if k < NSTEP - 1 else len(ORDER) + 4):
                        for stage, q, part in due(POOL_PARTS, position):
                            if not present(it, stage):
                                continue
                            g = it - 1
                            if stage == "LN1":
                                wait(pool, y1_stats, nth(g, q))
                                normalise(stats1, x1[:, q * QW:(q + 1) * QW], x1_ready)
                            elif stage == "KQ":
                                src = x1[:, q * QW:(q + 1) * QW]
                                dst = x1s[q % 3]
                                wait(pool, x1_ready, nth(g, q))
                                products_done(pool, it, "XT", q)
                                pool.tensor_tensor(dst[0][:], src, one[:].to_broadcast([128, QW]),
                                                   ALU.mult).then_inc(x1_hi, 1)
                                wait(pool, x1_hi, nth(g, q))
                                pool.tensor_tensor(dst[1][:], src, f32(dst[0][:]), ALU.subtract).then_inc(x1_split, 1)
                            elif stage == "SCORE":
                                wait(pool, exp_inverse, nth(g, q))
                                pool.tensor_tensor(quad(prob[:]), quad(expo[:]),
                                                   exp_inv[:].unsqueeze(2).to_broadcast([128, QB, 128]),
                                                   ALU.mult).then_inc(prob_ready, 1)
                            else:
                                wait(pool, y2_stats, nth(g, q))
                                normalise(stats2, y2[q % 2][:], y2_ready)
                        if position < len(ORDER) and ORDER[position][0] == "AGG1" and has_graph(it):
                            q = ORDER[position][1]
                            if q + 2 < NQ:
                                split_x(q + 2)
            iterations(pool, body)

        @block.scalar
        def _(act):
            def copy(dst, src, **kw):
                return act.activation(dst, src, ACT.Copy, **kw)

            for j, (kind, p) in enumerate(LSTM_JOBS):
                act.wait_ge(setup_pe, PE_LSTM + j)
                for a, b, s in GATE_PARTS:
                    copy(lstm_dst(kind, p, 0)[:, a * 128:b * 128], side_bank[j % 4][:, a * 128:b * 128],
                         scale=lstm_scale(kind, p, s)).then_inc(setup_act, 1)

            def side_part(it, stage, q, part):
                bank = side_bank[turn(it, stage, q)[0]][:]
                g = it + 1 if stage in GRAPH else it - 1
                done = act_hi[stage]
                if stage in ("AGG1", "AGG2", "XT", "VAL", "MIX"):
                    dst = {"AGG1": agg1, "AGG2": agg2, "XT": x1T[q % 2], "VAL": value[q % 2], "MIX": mix}[stage]
                    products_done(act, it, stage, q)
                    copy(dst[0][:], bank).then_inc(done, 1)
                elif stage == "KQ":
                    products_done(act, it, stage, q)
                    act.activation(query[0][:], bank, ACT.Identity, bias=key_bias[:, 0:1]).then_inc(done, 1)
                elif stage in ("PROJ1", "PROJ2"):
                    bank_read(act, it, stage, q)
                    src, dst = (sum1[:], h1[0][:]) if stage == "PROJ1" else (sum2[:], h2[0][:, q * QW:(q + 1) * QW])
                    act.activation(dst, src, ACT.Relu).then_inc(done, 1)
                elif part == "exp":
                    wait(act, score_max, nth(g, q))
                    for b in range(QB):
                        ins = act.activation(bat(expo, b), bat(score, b), ACT.Exp, bias=neg_max[:, b:b + 1],
                                             accum_out=exp_sum[:, b:b + 1])
                    ins.then_inc(exp_ready, 1)
                else:
                    wait(act, prob_ready, nth(g, q))
                    copy(probs[0][:], prob[:]).then_inc(done, 1)

            def body(it):
                for k, (p, c, s) in enumerate(STEPS):
                    first = FIRST[k]
                    last = FIRST[k + 1] if k < NSTEP - 1 else len(ORDER) + 4
                    if has_lstm(it):
                        for gate in (GI, GG, GF, GO):
                            if gate == GF and s == 0:
                                continue
                            wait(act, gate_ready[gate], gate_uses(it, gate, k) + 1)
                            act.activation(packed(gate_tile(k, gate), p), packed(gate_bank[gate], p), ACT.Tanh,
                                           bias=gate_bias[:, w_index(p, gate):w_index(p, gate) + 1]
                                           ).then_inc(gate_read[gate], 1)
                    for position in range(first, last):
                        if position == first + 1 and has_lstm(it):
                            wait(act, cell_ready, it * NSTEP + (k + 1))
                            act.activation(packed(cell_tanh, p), packed(cell[:, c % 2 * 512:(c % 2 + 1) * 512], p),
                                           ACT.Tanh, scale=0.5).then_inc(cell_tanh_ready, 1)
                        for stage, q, part in due(ACT_PARTS, position):
                            if present(it, stage):
                                side_part(it, stage, q, part)
                    if last == first + 1 and has_lstm(it):
                        wait(act, cell_ready, it * NSTEP + (k + 1))
                        act.activation(packed(cell_tanh, p), packed(cell[:, c % 2 * 512:(c % 2 + 1) * 512], p),
                                       ACT.Tanh, scale=0.5).then_inc(cell_tanh_ready, 1)
            iterations(act, body)

        @block.vector
        def _(dve):
            count = [0]

            def done(ins):
                count[0] += 1
                ins.then_inc(setup_dve, 1)

            def own():
                dve.wait_ge(setup_dve, count[0])

            ts, tt, stt, cp = dve.tensor_scalar, dve.tensor_tensor, dve.scalar_tensor_tensor, dve.tensor_copy
            dve.wait_ge(const_loaded, 16 * N_CONST)
            dve.wait_ge(setup_pe, PE_TRANSPOSED)
            done(cp(transposed, side_bank[0][:]))
            done(cp(bq_wide, bq_col.to_broadcast([128, 128])))
            done(cp(bv_wide, bv_col.to_broadcast([128, 128])))
            assert count[0] == DVE_WIDE
            done(dve.reduce_sum(row_sum, raw_at["adj"], AX.X))
            own()
            done(ts(parent, row_sum, 0.0, gamma_col, ALU.is_gt, ALU.mult))
            own()
            done(ts(keep, parent, -1.0, 1.0, ALU.mult, ALU.add))
            own()
            dve.wait_ge(setup_pool, 7)
            done(ts(diagonal, ident[:], keep, None, ALU.mult))
            own()
            done(stt(out=mixing, in0=raw_at["adj"], scalar=parent, in1=diagonal, op0=ALU.mult, op1=ALU.add))
            assert count[0] == DVE_AP
            dve.wait_ge(setup_pe, PE_MIXT)
            done(cp(mixT_f, side_bank[3][:, 0:128]))
            assert count[0] == DVE_MIXT
            dve.wait_ge(setup_pe, PE_SHIFTS)
            done(tt(shift_rows, side_bank[2][:, 0:128], raw_at["bo"], ALU.add))
            assert count[0] == DVE_SHIFT_ROWS
            dve.wait_ge(lstm_loaded, 64)
            done(tt(bih_rows, bih_rows, bhh_rows, ALU.add))
            assert count[0] == DVE_BIAS_ROWS
            done(ts(key_bias[:], side_bank[2][:, 128:129], SCALE, None, ALU.mult))
            done(ts(row_f, side_bank[2][:, 129:130].to_broadcast([128, 2]), SCALE, None, ALU.mult))
            done(ts(row_const, side_bank[2][:, 130:131], SCALE, None, ALU.mult))
            dve.wait_ge(setup_pe, PE_FOLDED)
            done(cp(bias1[:], side_bank[1][:, 0:128]))
            done(cp(bias2[:], side_bank[1][:, 128:256]))
            done(ts(kq[0][:], side_bank[1][:, 256:384], SCALE, None, ALU.mult))
            done(cp(vo[0][:], side_bank[1][:, 384:512]))
            own()
            done(tt(resT_f, mixT_f, ident[:], ALU.add))
            done(cp(row[0][:], row_f))
            done(cp(adjT[0][:], adjT_f))
            done(cp(wg0[0][:], raw_at["Wg0"]))
            done(cp(wg1[0][:], raw_at["Wg1"]))
            done(cp(mixT[0][:], mixT_f))
            done(ts(mask_bias[:], raw_at["adj"], 0.0, MASKED, ALU.is_equal, ALU.mult))
            own()
            done(cp(resT[0][:], resT_f))
            done(stt(out=kq[1][:], in0=side_bank[1][:, 256:384], scalar=SCALE, in1=f32(kq[0][:]),
                     op0=ALU.mult, op1=ALU.subtract))
            done(tt(vo[1][:], side_bank[1][:, 384:512], f32(vo[0][:]), ALU.subtract))
            done(tt(row[1][:], row_f, f32(row[0][:]), ALU.subtract))
            done(tt(adjT[1][:], adjT_f, f32(adjT[0][:]), ALU.subtract))
            done(tt(wg0[1][:], raw_at["Wg0"], f32(wg0[0][:]), ALU.subtract))
            done(tt(wg1[1][:], raw_at["Wg1"], f32(wg1[0][:]), ALU.subtract))
            done(tt(mixT[1][:], mixT_f, f32(mixT[0][:]), ALU.subtract))
            done(stt(out=mask_bias[:], in0=raw_at["adj"], scalar=alpha_col, in1=mask_bias[:], op0=ALU.mult, op1=ALU.add))
            own()
            done(tt(resT[1][:], resT_f, f32(resT[0][:]), ALU.subtract))
            done(ts(mask_bias[:], mask_bias[:], row_const, None, ALU.add))
            dve.wait_ge(setup_pe, PE_OUTBIAS)
            done(cp(out_bias[:], gate_bank[0][:, 0:128]))
            dve.wait_ge(setup_pe, PE_BIAS)
            done(ts(gate_bias[:], gate_bank[1][:, 0:16], 0.5, None, ALU.mult))
            own()
            done(cp(gate_bias[:, 2:16:4], gate_bank[1][:, 2:16:4]))
            for j, (kind, p) in enumerate(LSTM_JOBS):
                for n, (a, b, s) in enumerate(GATE_PARTS):
                    dve.wait_ge(setup_act, 3 * j + n + 1)
                    if n == 0:
                        dve.wait_ge(setup_act, 3 * (j + 1))
                    cols = slice(a * 128, b * 128)
                    done(stt(out=lstm_dst(kind, p, 1)[:, cols], in0=side_bank[j % 4][:, cols],
                             scalar=lstm_scale(kind, p, s), in1=f32(lstm_dst(kind, p, 0)[:, cols]),
                             op0=ALU.mult, op1=ALU.subtract))
            SETUP["dve"] = count[0]
            assert count[0] == SETUP_DVE, count[0]

            def side_part(it, stage, q, part):
                number, before = turn(it, stage, q)
                bank = side_bank[number][:]
                read = side_read[number]
                g = it + 1 if stage in GRAPH else it - 1
                if stage in ("AGG1", "AGG2", "XT", "VAL", "MIX"):
                    dst = {"AGG1": agg1, "AGG2": agg2, "XT": x1T[q % 2], "VAL": value[q % 2], "MIX": mix}[stage]
                    wait(dve, act_hi[stage], nth(g, q))
                    tt(dst[1][:], bank, f32(dst[0][:]), ALU.subtract).then_inc(read, 1)
                elif stage == "KQ":
                    wait(dve, act_hi[stage], nth(g, q))
                    stt(out=query[1][:], in0=bank, scalar=key_bias[:, 0:1], in1=f32(query[0][:]),
                        op0=ALU.add, op1=ALU.subtract).then_inc(read, 1)
                elif stage in ("PROJ1", "PROJ2"):
                    total, const = (sum1, bias1) if stage == "PROJ1" else (sum2, bias2)
                    if part == "sum":
                        products_done(dve, it, stage, q)
                        tt(quad(total[:]), quad(bank), spread(const[:]), ALU.add).then_inc(read, 1)
                    else:
                        hi, lo = ((h1[0][:], h1[1][:]) if stage == "PROJ1"
                                  else (h2[0][:, q * QW:(q + 1) * QW], h2[1][:, q * QW:(q + 1) * QW]))
                        wait(dve, act_hi[stage], nth(g, q))
                        stt(out=lo, in0=total[:], scalar=0.0, in1=f32(hi), op0=ALU.max, op1=ALU.subtract
                            ).then_inc(h1_split if stage == "PROJ1" else h2_split, 1)
                elif stage == "LN1":
                    dst = x1[:, q * QW:(q + 1) * QW]
                    wait(dve, x1_loaded[q], 16 * (g + 1))
                    products_done(dve, it, stage, q)
                    stt(out=dst, in0=bank, scalar=0.5, in1=dst, op0=ALU.mult, op1=ALU.add).then_inc(read, 1)
                    bank_read(dve, it, stage, q)
                    wait(dve, x1_ready, nth(g, q) - 1)
                    for b in range(QB):
                        ins = dve.bn_stats(stats1[:, b * 6:b * 6 + 6], bat(dst, b))
                    ins.then_inc(y1_stats, 1)
                elif stage == "ROW":
                    products_done(dve, it, stage, q)
                    cp(row_shift[:], bank[:, 0:2 * QB]).then_inc(read, 1)
                elif stage == "SCORE" and part == "sum":
                    products_done(dve, it, stage, q)
                    bank_read(dve, it, "ROW", q)
                    for b in range(QB):
                        ins = stt(out=bat(score, b), in0=bat(bank, b), scalar=row_shift[:, 2 * b:2 * b + 1],
                                  in1=mask_bias[:], op0=ALU.add, op1=ALU.add)
                    ins.then_inc(read, 1)
                    bank_read(dve, it, stage, q)
                    dve.tensor_reduce(neg_max[:], quad(score[:]), AX.X, ALU.max, negate=True).then_inc(score_max, 1)
                elif stage == "SCORE" and part == "inv":
                    wait(dve, exp_ready, nth(g, q))
                    dve.reciprocal(exp_inv[:], exp_sum[:]).then_inc(exp_inverse, 1)
                elif stage == "SCORE":
                    wait(dve, act_hi[stage], nth(g, q))
                    tt(probs[1][:], prob[:], f32(probs[0][:]), ALU.subtract).then_inc(prob_split, 1)
                else:
                    dst = y2[q % 2]
                    products_done(dve, it, stage, q)
                    wait(dve, y2_stored[q % 2], 16 * (g * 2 + q // 2))
                    tt(quad(dst[:]), quad(bank), spread(out_bias[:]), ALU.add).then_inc(read, 1)
                    bank_read(dve, it, stage, q)
                    wait(dve, y2_ready, nth(g, q) - 1)
                    for b in range(QB):
                        ins = dve.bn_stats(stats2[:, b * 6:b * 6 + 6], bat(dst, b))
                    ins.then_inc(y2_stats, 1)

            def new_cell(it, k):
                p, c, s = STEPS[k]
                ti, tf, tg = (packed(gate_tile(k, g), p) for g in (GI, GF, GG))
                old = packed(cell[:, c % 2 * 512:(c % 2 + 1) * 512], p)
                terms = sum(1 for _, _, s_ in STEPS if s_)
                before = 2 * (it * terms + sum(1 for _, _, s_ in STEPS[:k] if s_))
                wait(dve, gate_read[GG], gate_uses(it, GG, k) + 1)
                if s == 0:
                    stt(out=old, in0=ti, scalar=1.0, in1=tg, op0=ALU.add, op1=ALU.mult).then_inc(cell_ready, 1)
                    return
                stt(out=ti, in0=ti, scalar=1.0, in1=tg, op0=ALU.add, op1=ALU.mult).then_inc(cell_term, 1)
                wait(dve, gate_read[GF], gate_uses(it, GF, k) + 1)
                stt(out=tf, in0=tf, scalar=1.0, in1=old, op0=ALU.add, op1=ALU.mult).then_inc(cell_term, 1)
                wait(dve, cell_term, before + 2)
                stt(out=old, in0=tf, scalar=0.5, in1=ti, op0=ALU.mult, op1=ALU.add).then_inc(cell_ready, 1)

            def new_hidden(it, k):
                p, c, s = STEPS[k]
                to = packed(gate_tile(k, GO), p)
                kept = s == p - 1
                full = window(final, p, c, s) if kept else packed(fresh, p)
                wait(dve, gate_read[GO], gate_uses(it, GO, k) + 1)
                wait(dve, cell_tanh_ready, it * NSTEP + (k + 1))
                stt(out=full, in0=to, scalar=1.0, in1=packed(cell_tanh, p), op0=ALU.add, op1=ALU.mult
                    ).then_inc(h_full, 1)
                if k < NSPLIT:
                    hi, lo = ((window(t, p, c, s) for t in state) if kept else (packed(t, p) for t in hidden[c]))
                    wait(dve, h_full, it * NSTEP + (k + 1))
                    cp(hi, full).then_inc(h_hi, 1)
                    wait(dve, h_hi, it * NSPLIT + (k + 1))
                    tt(lo, full, f32(hi), ALU.subtract).then_inc(h_split, 1)

            def body(it):
                for k in range(NSTEP):
                    first = FIRST[k]
                    last = FIRST[k + 1] if k < NSTEP - 1 else len(ORDER) + 4
                    if has_lstm(it):
                        new_cell(it, k)
                    for position in range(first, last):
                        if position == first + 1 and has_lstm(it):
                            new_hidden(it, k)
                        for stage, q, part in due(DVE_PARTS, position):
                            if present(it, stage):
                                side_part(it, stage, q, part)
                    if last == first + 1 and has_lstm(it):
                        new_hidden(it, k)
            iterations(dve, body)

        @block.tensor
        def _(pe):
            def mm(dst, lhsT, rhs, start, stop):
                return nc.tensor.matmul(dst, lhsT, rhs, start=start, stop=stop)

            pe.wait_ge(const_loaded, 16 * N_CONST)
            pe.wait_ge(setup_pool, 7)
            for i, name in enumerate(("adj", "Wq", "Wk", "Wv")):
                ins = nc.tensor.transpose(bat(side_bank[0], i), raw_at[name], ident[:])
            ins.then_inc(setup_pe, 1)
            pe.wait_ge(setup_dve, DVE_WIDE)
            mm(side_bank[1][:, 0:128], adjT_f, raw_at["bg0"], True, True)
            mm(side_bank[1][:, 128:256], raw_at["bg1"], adjT_f, True, True)
            mm(side_bank[1][:, 256:384], wqT, wkT, True, True)
            mm(side_bank[1][:, 384:512], wvT, raw_at["Wo"], True, True).then_inc(setup_pe, 1)
            mm(side_bank[2][:, 0:128], bv_wide, raw_at["Wo"], True, True)
            mm(side_bank[2][:, 128:129], wkT, bq_col, True, True)
            mm(side_bank[2][:, 129:130], wqT, bk_col, True, True)
            mm(side_bank[2][:, 130:131], bq_wide, bk_col, True, True).then_inc(setup_pe, 1)
            pe.wait_ge(setup_dve, DVE_AP)
            nc.tensor.transpose(side_bank[3][:, 0:128], mixing, ident[:]).then_inc(setup_pe, 1)
            pe.wait_ge(setup_dve, DVE_SHIFT_ROWS)
            mm(gate_bank[0][:, 0:128], mixT_f, shift_rows, True, True).then_inc(setup_pe, 1)
            pe.wait_ge(setup_dve, DVE_BIAS_ROWS)
            nc.tensor.transpose(gate_bank[1][:, 0:16], bih_rows, ident[0:16, 0:16]).then_inc(setup_pe, 1)
            pe.wait_ge(setup_dve, SETUP_DVE - 3 * len(LSTM_JOBS))
            for j, (kind, p) in enumerate(LSTM_JOBS):
                if j >= 4:
                    pe.wait_ge(setup_dve, SETUP_DVE - 3 * (len(LSTM_JOBS) - j + 3))
                src = raw_ih if kind == "ih" else raw_hh
                for gate in range(4):
                    ins = nc.tensor.transpose(bat(side_bank[j % 4], gate), bat(src, w_index(p, gate)), ident[:])
                ins.then_inc(setup_pe, 1)
            pe.wait_ge(setup_dve, SETUP_DVE)

            def three(dst, a, b, start, stop):
                mm(dst, a[0], b[0], start, False)
                mm(dst, a[0], b[1], False, False)
                return mm(dst, a[1], b[0], False, stop)

            def both(pair, cut):
                return [cut(t) for t in pair]

            def side_job(it, stage, q):
                number, before = turn(it, stage, q)
                bank = side_bank[number]
                g = it + 1 if stage in GRAPH else it - 1
                wait(pe, side_read[number], before)

                def per_batch(a, b_of):
                    for i in range(QB):
                        ins = three(bat(bank, i), both(a, lambda t: bat(t, i)), b_of(i), True, True)
                    return ins

                if stage == "AGG1":
                    wait(pe, x_split, nth(g, q))
                    ins = per_batch(xs[q % 2], lambda i: both(adjT, lambda t: t[:]))
                elif stage == "PROJ1":
                    bank_read(pe, it, "AGG1", q)
                    ins = per_batch(agg1, lambda i: both(wg0, lambda t: t[:]))
                elif stage == "AGG2":
                    wait(pe, h1_split, nth(g, q))
                    ins = per_batch(h1, lambda i: both(adjT, lambda t: t[:]))
                elif stage == "PROJ2":
                    bank_read(pe, it, "AGG2", q)
                    ins = three(bank[:], both(wg1, lambda t: t[:]), both(agg2, lambda t: t[:]), True, True)
                elif stage == "LN1":
                    wait(pe, h_full, NSTEP * (g + 1))
                    for i in range(QB):
                        ins = nc.tensor.transpose(bat(bank, i), bat(final, q * QB + i), ident[:])
                elif stage == "XT":
                    wait(pe, x1_ready, nth(g, q))
                    for i in range(QB):
                        ins = nc.tensor.transpose(bat(bank, i), bat(x1, q * QB + i), ident[:])
                elif stage == "KQ":
                    bank_read(pe, it, "XT", q)
                    ins = three(bank[:], both(kq, lambda t: t[:]), both(x1T[q % 2], lambda t: t[:]), True, True)
                elif stage == "VAL":
                    ins = per_batch(x1T[q % 2], lambda i: both(vo, lambda t: t[:]))
                elif stage == "ROW":
                    for i in range(QB):
                        ins = three(bank[:, 2 * i:2 * i + 2], both(x1T[q % 2], lambda t: bat(t, i)),
                                    both(row, lambda t: t[:]), True, True)
                elif stage == "SCORE":
                    bank_read(pe, it, "KQ", q)
                    ins = per_batch(query, lambda i: both(x1T[q % 2], lambda t: bat(t, i)))
                elif stage == "MIX":
                    wait(pe, prob_split, nth(g, q))
                    ins = per_batch(probs, lambda i: both(mixT, lambda t: t[:]))
                else:
                    wait(pe, x1_split, nth(g, q))
                    bank_read(pe, it, "MIX", q)
                    bank_read(pe, it, "VAL", q)
                    three(bank[:], both(resT, lambda t: t[:]), both(x1s[q % 3], lambda t: t[:]), True, False)
                    for i in range(QB):
                        ins = three(bat(bank, i), both(mix, lambda t: bat(t, i)),
                                    both(value[q % 2], lambda t: bat(t, i)), False, i == QB - 1)
                ins.then_inc(side_ready[number], 1)

            def lstm_step(it, k):
                p, c, s = STEPS[k]
                used = [g for g in (GI, GG, GF, GO) if g != GF or s > 0]
                if p == 1:
                    wait(pe, h2_split, nth(it, c))
                    inputs = both(h2, lambda t: window(t, 1, c, 0))
                else:
                    parents = [j for j in range(k) if STEPS[j][0] < p]
                    wait(pe, h_split, it * NSPLIT + (max(parents) + 1))
                    inputs = both(state, lambda t: window(t, p, c, s))
                for gate in used:
                    at = w_index(p, gate)
                    wait(pe, gate_read[gate], gate_uses(it, gate, k))
                    ins = three(packed(gate_bank[gate], p), both(wih, lambda t: bat(t, at)), inputs, True, s == 0)
                    if s == 0:
                        ins.then_inc(gate_ready[gate], 1)
                if s > 0:
                    wait(pe, h_split, it * NSPLIT + (STEPS.index((p, c, s - 1)) + 1))
                    for gate in used:
                        at = (p - 2) * 4 + gate
                        three(packed(gate_bank[gate], p), both(whh, lambda t: bat(t, at)),
                              both(hidden[c], lambda t: packed(t, p)), False, True).then_inc(gate_ready[gate], 1)

            def body(it):
                for k in range(NSTEP):
                    if has_lstm(it):
                        lstm_step(it, k)
                    for stage, q in FILL[k]:
                        if present(it, stage):
                            side_job(it, stage, q)
            iterations(pe, body)


_INS = ['x', 'adj', 'L0_gnn_Wg0', 'L0_gnn_bg0', 'L0_gnn_Wg1', 'L0_gnn_bg1', 'L0_gnn_Wih', 'L0_gnn_Whh',
        'L0_gnn_bih', 'L0_gnn_bhh', 'L1_gnn_Wq', 'L1_gnn_bq', 'L1_gnn_Wk', 'L1_gnn_bk', 'L1_gnn_Wv',
        'L1_gnn_bv', 'L1_gnn_Wo', 'L1_gnn_bo', 'L1_gnn_alpha', 'L1_gnn_gamma']


def kernel(**inputs):
    import numpy as _np
    import concourse.bacc as _bacc
    from concourse import mybir as _mybir
    from concourse.bass_utils import run_bass_kernel_spmd as _run

    nc = _bacc.Bacc("TRN2", target_bir_lowering=False, num_devices=1)
    arrays, args = {}, []
    for name in _INS:
        a = _np.ascontiguousarray(inputs[name]).reshape(_np.shape(inputs[name]) or (1,))
        arrays[f"in_{name}_dram"] = a
        args.append(nc.dram_tensor(f"in_{name}_dram", a.shape, _mybir.dt.from_np(a.dtype), kind="ExternalInput").ap())
    args.append(nc.dram_tensor("out_0_dram", (NB, T, D), F32, kind="ExternalOutput").ap())
    graph_resnorm_kernel(nc, *args)
    r = _run(nc, [arrays], core_ids=[0])
    return r.results[0]["out_0_dram"]
```

```python
from contextlib import ExitStack

import concourse.bass as bass
from concourse import mybir

F32 = mybir.dt.float32
F32R = mybir.dt.float32r
ALU = mybir.AluOpType
ACT = mybir.ActivationFunctionType
AX = mybir.AxisListType

NB, T, D = 128, 128, 128
GB, QB = 16, 4
NG, NQ = NB // GB, GB // QB
QW = QB * T
GW = GB * T
MAX_SKIP = 4
EPS = 1e-5
MASKED = -1e30
SCALE = float(D) ** -0.5


GI, GF, GG, GO = range(4)

STEPS = ([(1, 0, 0), (4, 0, 0), (1, 1, 0), (4, 0, 1), (1, 2, 0), (4, 0, 2), (1, 3, 0), (4, 0, 3)]
         + [(2, c, s) for s in range(2) for c in range(2)]
         + [(3, c, s) for s in range(3) for c in range(2)])
NCHUNK = {1: 4, 2: 2, 3: 2, 4: 1}
NSTEP = len(STEPS)

FILL = [
    [("PROJ2", 2, 0), ("VAL", 0, 2)],
    [("AGG2", 3, 0), ("PT", 0, 2), ("LN1", 3, 2)],
    [("VAL", 1, 2), ("SCORE", 1, 2), ("XT", 2, 2)],
    [("PROJ2", 3, 0), ("PV", 0, 2)],
    [("KQ", 2, 2), ("AGG1", 0, -1)],
    [("VAL", 2, 2), ("PT", 1, 2)],
    [("PROJ1", 0, -1), ("XT", 3, 2), ("OUT", 0, 2)],
    [("PV", 1, 2), ("SCORE", 2, 2), ("KQ", 3, 2)],
    [("AGG1", 1, -1), ("AGG2", 0, -1), ("LN1", 0, 1)],
    [("VAL", 3, 2), ("PROJ1", 1, -1), ("OUT", 1, 2)],
    [("PT", 2, 2), ("SCORE", 3, 2)],
    [("XT", 0, 1)],
    [("PROJ2", 0, -1), ("PV", 2, 2), ("AGG1", 2, -1), ("AGG2", 1, -1)],
    [("LN1", 1, 1)],
    [("PROJ1", 2, -1), ("KQ", 0, 1), ("PT", 3, 2)],
    [("OUT", 2, 2), ("PROJ2", 1, -1), ("PV", 3, 2)],
    [("XT", 1, 1), ("SCORE", 0, 1), ("AGG1", 3, -1), ("AGG2", 2, -1)],
    [("PROJ1", 3, -1), ("OUT", 3, 2), ("KQ", 1, 1), ("LN1", 2, 1)],
]
LOOP_FIRST, LOOP_ROUNDS = 3, 2
ORDER = [job for slot in FILL for job in slot]
PLACE = {(stage, q): n for n, (stage, q, _) in enumerate(ORDER)}
FIRST = [sum(len(s) for s in FILL[:k]) for k in range(NSTEP + 1)]
GRAPH = ("AGG1", "PROJ1", "AGG2", "PROJ2")

EARLY, LATE = range(2)
ACT_PARTS = {
    "AGG1": [("hi", 0, LATE)],
    "PROJ1": [("hi", 1, EARLY)],
    "AGG2": [("hi", 0, LATE)],
    "PROJ2": [("hi", 1, EARLY)],
    "XT": [("hi", 0, LATE)],
    "KQ": [("hi", 0, LATE), ("shift", 2, LATE)],
    "VAL": [("hi", 0, LATE)],
    "SCORE": [("exp", 1, LATE)],
    "PT": [("hi", 0, LATE)],
    "PV": [("hi", 1, EARLY)],
}
DVE_PARTS = {
    "AGG1": [("lo", 0, LATE)],
    "PROJ1": [("sum", 0, EARLY), ("lo", 1, EARLY)],
    "AGG2": [("lo", 0, LATE)],
    "PROJ2": [("sum", 0, LATE), ("lo", 1, EARLY)],
    "LN1": [("sum", 1, EARLY)],
    "XT": [("lo", 0, LATE)],
    "KQ": [("lo", 0, LATE)],
    "VAL": [("lo", 0, LATE)],
    "SCORE": [("sum", 0, LATE), ("inv", 1, LATE)],
    "PT": [("lo", 0, LATE)],
    "PV": [("sum", 0, EARLY), ("lo", 1, EARLY)],
    "OUT": [("sum", 0, LATE)],
}
POOL_PARTS = {
    "AGG1": [("split", -4, LATE)],
    "LN1": [("norm", 0, LATE)],
    "KQ": [("prepare", 0, LATE)],
    "SCORE": [("norm", 1, LATE)],
    "OUT": [("norm", 2, LATE)],
}
SP_PARTS = {
    "AGG1": [("load", -4, LATE)],
    "OUT": [("load", 1, LATE), ("store", 2, LATE)],
}


def due(parts, k, when=LATE):
    found = []
    for later in range(3, -5, -1):
        step, wrap = (k - later) % NSTEP, -((k - later) // NSTEP)
        for place in range(FIRST[step], FIRST[step + 1]):
            found += [(place, wrap, part) for part, steps, at in parts.get(ORDER[place][0], [])
                      if steps == later and at == when]
    return found


def graph_resnorm_kernel(nc, x, adj, Wg0, bg0, Wg1, bg1, Wih, Whh, bih, bhh,
                         Wq, bq, Wk, bk, Wv, bv, Wo, bo, alpha, gamma, out):
    with ExitStack() as ctx:
        def sb(name, cols, dt=F32, rows=128):
            return ctx.enter_context(nc.sbuf_tensor(name, [rows, cols], dt))

        def sem(name):
            return ctx.enter_context(nc.semaphore(name))

        def quad(ap):
            return ap.rearrange("p (b t) -> p b t", b=QB)

        def spread(ap):
            return ap.unsqueeze(1).to_broadcast([128, QB, 128])

        gate_bank = [ctx.enter_context(nc.psum_tensor(f"gate_bank{i}", [128, 512], F32)) for i in range(4)]
        side_bank = [ctx.enter_context(nc.psum_tensor(f"side_bank{i}", [128, 512], F32)) for i in range(4)]

        ident = sb("ident", 128)
        adjT = [sb(f"adjT_{h}", 128, F32R) for h in ("hi", "lo")]
        wg0 = [sb(f"wg0_{h}", 128, F32R) for h in ("hi", "lo")]
        wg1 = [sb(f"wg1_{h}", 128, F32R) for h in ("hi", "lo")]
        kq = [sb(f"kq_{h}", 128, F32R) for h in ("hi", "lo")]
        vo = [sb(f"vo_{h}", 128, F32R) for h in ("hi", "lo")]
        query_row = sb("query_row", 128)
        mixT = [sb(f"mixT_{h}", 128, F32R) for h in ("hi", "lo")]
        wih = [sb(f"wih_{h}", 16 * 128, F32R) for h in ("hi", "lo")]
        whh = [sb(f"whh_{h}", 12 * 128, F32R) for h in ("hi", "lo")]
        gate_bias = sb("gate_bias", 16)
        bias1 = sb("bias1", 128)
        bias2 = sb("bias2", 128)
        key_bias = sb("key_bias", 1)
        mask_bias = sb("mask_bias", 128)
        out_bias = sb("out_bias", 128)
        half = sb("half", 8)
        one = sb("one", 1)
        inv_d = sb("inv_d", 4)
        eps = sb("eps", 4)
        neg_half = sb("neg_half", 4)

        xg = sb("xg", GW)
        xs = [[sb(f"xs{n}_{h}", QW, F32R) for h in ("hi", "lo")] for n in range(2)]
        agg1 = [sb(f"agg1_{h}", QW, F32R) for h in ("hi", "lo")]
        sum1 = sb("sum1", QW)
        h1 = [sb(f"h1_{h}", QW, F32R) for h in ("hi", "lo")]
        agg2 = [sb(f"agg2_{h}", QW, F32R) for h in ("hi", "lo")]
        sum2 = sb("sum2", QW)

        state = [[sb(f"state{n}_{h}", GW, F32R) for h in ("hi", "lo")] for n in range(2)]
        gates = sb("gates", 2 * 4 * 512)
        final = [sb(f"final{n}", GW) for n in range(2)]
        cell = sb("cell", 2 * 512)
        cell_tanh = sb("cell_tanh", 512)
        fresh = sb("fresh", 512)
        hidden = [[sb(f"hidden{n}_{h}", 512, F32R) for h in ("hi", "lo")] for n in range(2)]

        x1 = sb("x1", GW)
        stats1 = sb("stats1", NQ * QB * 6)
        stats2 = sb("stats2", NQ * QB * 6)
        moments = sb("moments", 8 * 4)
        x1T = [[sb(f"x1T{n}_{h}", QW, F32R) for h in ("hi", "lo")] for n in range(2)]
        query = [sb(f"query_{h}", QW, F32R) for h in ("hi", "lo")]
        value = [[sb(f"value{n}_{h}", QW, F32R) for h in ("hi", "lo")] for n in range(2)]
        row_product = sb("row_product", QW)
        row_shift = sb("row_shift", NQ * QB)
        score = sb("score", QW)
        neg_max = sb("neg_max", QB)
        expo = sb("expo", QW)
        exp_sum = sb("exp_sum", QB)
        exp_inv = sb("exp_inv", QB)
        prob = sb("prob", QW)
        probT = [sb(f"probT_{h}", QW, F32R) for h in ("hi", "lo")]
        refined = sb("refined", QW)
        refined_parts = [sb(f"refined_{h}", QW, F32R) for h in ("hi", "lo")]
        y2 = [sb(f"y2_{n}", QW) for n in range(NQ)]

        const_loaded = sem("const_loaded")
        lstm_loaded = sem("lstm_loaded")
        setup_pe = sem("setup_pe")
        weights_transposed = sem("weights_transposed")
        weights_hi = sem("weights_hi")
        weights_lo = sem("weights_lo")
        setup_dve = sem("setup_dve")
        setup_pool = sem("setup_pool")
        xg_loaded = [sem(f"xg_loaded{q}") for q in range(NQ)]
        x1_loaded = [sem(f"x1_loaded{q}") for q in range(NQ)]
        y2_stored = [sem(f"y2_stored{q}") for q in range(NQ)]
        gate_ready = [sem(f"gate_ready{i}") for i in range(4)]
        gate_read = [sem(f"gate_read{i}") for i in range(4)]
        side_ready = [sem(f"side_ready{i}") for i in range(4)]
        side_read = [sem(f"side_read{i}") for i in range(4)]
        cell_term = sem("cell_term")
        cell_ready = sem("cell_ready")
        cell_tanh_ready = sem("cell_tanh_ready")
        h_full = sem("h_full")
        h_hi = sem("h_hi")
        h_split = sem("h_split")
        act_hi = {s: sem(f"hi_{s}") for s in ("AGG1", "PROJ1", "AGG2", "PROJ2", "XT", "KQ", "VAL", "PT", "PV")}
        x_hi = sem("x_hi")
        x_split = sem("x_split")
        pool_step = sem("pool_step")
        h1_split = sem("h1_split")
        h2_split = sem("h2_split")
        y1_ready = sem("y1_ready")
        y1_stats = sem("y1_stats")
        x1_ready = sem("x1_ready")
        row_product_ready = sem("row_product_ready")
        row_ready = sem("row_ready")
        y2_base = sem("y2_base")
        score_max = sem("score_max")
        exp_ready = sem("exp_ready")
        exp_inverse = sem("exp_inverse")
        prob_ready = sem("prob_ready")
        refined_split = sem("refined_split")
        y2_stats = sem("y2_stats")
        y2_ready = sem("y2_ready")

        def f32(ap):
            return ap.bitcast(F32)

        def wait(eng, s, value):
            if not isinstance(value, int) or value > 0:
                eng.wait_ge(s, value)

        def nth(group, q):
            return group * NQ + (q + 1)

        def counted(it, f):
            if isinstance(it, int):
                return f(it)
            first = f(LOOP_FIRST)
            rate = f(LOOP_FIRST + 1) - first
            assert all(f(LOOP_FIRST + n) == first + n * rate for n in range(2 * LOOP_ROUNDS))
            return it * rate + (first - LOOP_FIRST * rate)

        def quad_stats(stats, q, b):
            at = (q * QB + b) * 6
            return stats[:, at:at + 6]

        def bat(ap, b):
            return ap[:, b * 128:(b + 1) * 128]

        def group_of(job):
            it, _, place, wrap = job
            return it - (wrap + ORDER[place][2])

        def parity_of(job):
            _, parity, place, wrap = job
            return (parity - wrap - ORDER[place][2]) % 2

        def in_range(group):
            return not isinstance(group, int) or 0 <= group < NG

        def present(job):
            return in_range(group_of(job))

        def latest(job, stage, q):
            it, parity, place, wrap = job
            return it, parity, PLACE[stage, q], wrap + (PLACE[stage, q] > place)

        def jobs_before(it, place):
            return sum(1 for t in range(-1, it + 1) for n, (_, _, lag) in enumerate(ORDER)
                       if 0 <= t - lag < NG and (t < it or n < place))

        def turn(job):
            it, _, place, wrap = job
            bank = jobs_before((it if isinstance(it, int) else LOOP_FIRST) - wrap, place) % 4
            return bank, counted(it, lambda t: jobs_before(t - wrap, place) // 4)

        def products_done(eng, job):
            bank, before = turn(job)
            wait(eng, side_ready[bank], before + 1)

        def bank_read(eng, job):
            bank, before = turn(job)
            wait(eng, side_read[bank], before + 1)

        def step_group(it, k):
            return it - (STEPS[k][0] == 4)

        def has_step(it, k):
            return in_range(step_group(it, k))

        def steps_before(it, k, kind=lambda step: True):
            return counted(it, lambda t: sum(
                1 for u in range(0, t + 1) for n, step in enumerate(STEPS)
                if kind(step) and has_step(u, n) and (u < t or n < k)))

        def is_split(step):
            return step != (4, 0, 3)

        def splits_before(it, k):
            return steps_before(it, k, is_split)

        def gate_uses(it, gate, k):
            return steps_before(it, k, lambda step: gate != GF or step[2] > 0)

        def lane(p, chunk):
            return {1: 0, 4: 1}.get(p, chunk)

        def cell_of(p, chunk):
            return packed(cell[:, lane(p, chunk) * 512:(lane(p, chunk) + 1) * 512], p)

        def window(tile, p, chunk, s):
            nb = GB // NCHUNK[p]
            nw = T // p
            return tile[:, chunk * nb * T:(chunk + 1) * nb * T].rearrange(
                "h (b t) -> h b t", b=nb)[:, :, s:s + p * (nw - 1) + 1:p]

        def packed(tile, p):
            nb = GB // NCHUNK[p]
            nw = T // p
            return tile[:, 0:nb * nw].rearrange("h (b w) -> h b w", b=nb)

        def gate_tile(it, k, gate):
            turn_of = steps_before(it if isinstance(it, int) else LOOP_FIRST, k) % 2
            at = (turn_of * 4 + gate) * 512
            return gates[:, at:at + 512]

        def w_index(p, gate):
            return (p - 1) * 4 + gate

        raw_ih, raw_hh = final
        raw = gates
        raw_at = {n: raw[:, i * 128:(i + 1) * 128] for i, n in enumerate(
            ("adj", "Wq", "Wk", "Wv", "Wo", "Wg0", "Wg1", "bg0", "bg1", "bo"))}
        transposed = raw[:, 1280:1792]
        adjT_f, wqT, wkT, wvT = (transposed[:, i * 128:(i + 1) * 128] for i in range(4))
        bq_wide = raw[:, 1792:1920]
        bv_wide = raw[:, 1920:2048]
        mixing = raw[:, 2048:2176]
        diagonal = raw[:, 2176:2304]
        mixT_f = raw[:, 2304:2432]
        bk_wide = raw[:, 2432:2560]
        shift_rows = raw[:, 2560:2688]
        columns = raw[:, 2688:2704]
        bq_col, bk_col, bv_col, alpha_col, gamma_col = (columns[:, i:i + 1] for i in range(5))
        row_sum, parent, keep, row_const = (columns[:, i:i + 1] for i in range(5, 9))
        bih_rows = raw[0:16, 2816:2944]
        bhh_rows = raw[0:16, 2944:3072]

        N_CONST = 15
        (PE_TRANSPOSED, PE_FOLDED, PE_SHIFTS, PE_MIXT, PE_OUTBIAS) = range(1, 6)
        PE_BIAS = 6
        LSTM_JOBS = [("ih", 1), ("ih", 2), ("ih", 3), ("ih", 4), ("hh", 2), ("hh", 3), ("hh", 4)]
        GATE_PARTS = [(0, 2, 0.5), (2, 3, 1.0), (3, 4, 0.5)]
        DVE_TRANSPOSED, DVE_WIDE = 1, 4

        def lstm_scale(kind, p, s):
            return s if kind == "ih" and p == 1 else 0.5 * s

        def lstm_dst(kind, p, half_index):
            w, base = (wih, (p - 1) * 4) if kind == "ih" else (whh, (p - 2) * 4)
            return w[half_index][:, base * 128:(base + 4) * 128]

        DVE_AP = 9
        DVE_MIXT = 10
        DVE_SHIFT_ROWS = 11
        DVE_BIAS_ROWS = 12
        SETUP_DVE = 35
        FIRST_WEIGHTS = 3

        def weights_due(it, k):
            j = k - FIRST_WEIGHTS
            return [j] if isinstance(it, int) and it == -1 and 0 <= j < len(LSTM_JOBS) else []

        block = ctx.enter_context(nc.Block())

        def iterations(eng, body):
            for it in range(-1, LOOP_FIRST):
                body(it, it % 2)
            with eng.Fori(0, LOOP_ROUNDS) as pair:
                body(pair * 2 + LOOP_FIRST, LOOP_FIRST % 2)
                body(pair * 2 + (LOOP_FIRST + 1), (LOOP_FIRST + 1) % 2)
            for it in range(LOOP_FIRST + 2 * LOOP_ROUNDS, NG + 3):
                body(it, it % 2)

        x_quads = x.rearrange("(n b) t d -> n t b d", b=QB)
        out_quads = out.rearrange("(n b) t d -> n t b d", b=QB)

        @block.sync
        def _(sp):
            def load_const(dst, src):
                sp.dma_start(dst, src).then_inc(const_loaded, 16)

            with nc.allow_non_contiguous_dma(reason="bias columns, 4 bytes each"):
                load_const(raw_at["adj"], adj)
                for name, w in (("Wq", Wq), ("Wk", Wk), ("Wv", Wv), ("Wo", Wo), ("Wg0", Wg0), ("Wg1", Wg1)):
                    load_const(raw_at[name], w)
                for name, b in (("bg0", bg0), ("bg1", bg1), ("bo", bo)):
                    load_const(raw_at[name], b.rearrange("(a d) -> a d", a=1).to_broadcast([128, 128]))
                for col, b in ((bq_col, bq), (bk_col, bk), (bv_col, bv)):
                    load_const(col, b.rearrange("(d a) -> d a", a=1))
                for col, b in ((alpha_col, alpha), (gamma_col, gamma)):
                    load_const(col, b.rearrange("(a d) -> a d", a=1).to_broadcast([128, 1]))
                for q in range(NQ):
                    sp.dma_start(quad(xg[:, q * QW:(q + 1) * QW]), x_quads[q]).then_inc(xg_loaded[q], 16)
                sp.dma_start(raw_ih[:].rearrange("r (g h) -> r g h", g=16),
                             Wih.rearrange("p (g r) h -> r (p g) h", g=4)).then_inc(lstm_loaded, 16)
                sp.dma_start(raw_hh[:].rearrange("r (g h) -> r g h", g=16),
                             Whh.rearrange("p (g r) h -> r (p g) h", g=4)).then_inc(lstm_loaded, 16)
                sp.dma_start(bih_rows, bih.rearrange("p (g h) -> (p g) h", g=4)).then_inc(lstm_loaded, 16)
                sp.dma_start(bhh_rows, bhh.rearrange("p (g h) -> (p g) h", g=4)).then_inc(lstm_loaded, 16)

                for q in range(NQ):
                    sp.dma_start(quad(x1[:, q * QW:(q + 1) * QW]), x_quads[q]).then_inc(x1_loaded[q], 16)

            def body(it, parity):
                for k in range(NSTEP):
                    for place, wrap, part in due(SP_PARTS, k):
                        job = (it, parity, place, wrap)
                        stage, q, _ = ORDER[place]
                        g = group_of(job)
                        cols = slice(q * QW, (q + 1) * QW)
                        if not present(job):
                            continue
                        if stage == "AGG1":
                            if isinstance(g, int) and g == 0:
                                continue
                            wait(sp, x_split, nth(g - 1, q))
                            sp.dma_start(quad(xg[:, cols]), x_quads[g * NQ + q]).then_inc(xg_loaded[q], 16)
                        elif part == "load":
                            if not in_range(g + 1):
                                continue
                            bank_read(sp, job)
                            sp.dma_start(quad(x1[:, cols]), x_quads[(g + 1) * NQ + q]).then_inc(x1_loaded[q], 16)
                        else:
                            wait(sp, y2_ready, nth(g, q))
                            sp.dma_start(out_quads[g * NQ + q], quad(y2[q][:])).then_inc(y2_stored[q], 16)
            iterations(sp, body)
            for q in range(NQ):
                sp.wait_ge(y2_stored[q], 16 * NG)

        @block.gpsimd
        def _(pool):
            pool.memset(half[:], 0.5).then_inc(setup_pool, 1)
            pool.memset(one[:], 1.0).then_inc(setup_pool, 1)
            pool.memset(inv_d[:], 1.0 / D).then_inc(setup_pool, 1)
            pool.memset(eps[:], EPS).then_inc(setup_pool, 1)
            pool.memset(neg_half[:], -0.5).then_inc(setup_pool, 1)
            pool.memset(ident[:], 0.0).then_inc(setup_pool, 1)
            pool.wait_ge(setup_pool, 6)
            pool.affine_select(out=ident[:], in_=ident[:], compare_op=ALU.not_equal, fill=1.0,
                               base=0, pattern=[[-1, 128]], channel_multiplier=1).then_inc(setup_pool, 1)

            chain_length = 6
            norms = [0]

            def body(it, parity):
                if isinstance(it, int) and it == LOOP_FIRST + 2 * LOOP_ROUNDS:
                    norms[0] += (LOOP_ROUNDS - 1) * 2 * 2 * NQ

                def step(ins, n):
                    ins.then_inc(pool_step, 1)
                    done = norms[0] * chain_length + n
                    if not isinstance(it, int):
                        done = it * (2 * NQ * chain_length) + (done - (LOOP_FIRST + (parity != LOOP_FIRST % 2)) * 2 * NQ * chain_length)
                    pool.wait_ge(pool_step, done)

                def normalise(stats, q, tile, ready):
                    st = stats[:, q * QB * 6:(q + 1) * QB * 6].rearrange("p (b s) -> p b s", s=6)
                    m = moments[:].rearrange("p (k b) -> p k b", b=QB)
                    pair = moments[:, 0:8].rearrange("p (k b) -> p b k", b=QB)
                    tt = pool.tensor_tensor
                    tt(m[:, 4], st[:, :, 2], st[:, :, 5], ALU.add)
                    step(tt(pair, st[:, :, 1:5:3], half[:].rearrange("p (b k) -> p b k", b=QB), ALU.mult), 1)
                    tt(m[:, 5], m[:, 4], inv_d[:], ALU.mult)
                    tt(m[:, 2], m[:, 0], m[:, 1], ALU.add)
                    step(tt(m[:, 3], m[:, 0], m[:, 1], ALU.subtract), 2)
                    tt(m[:, 4], m[:, 5], eps[:], ALU.add)
                    step(tt(m[:, 6], m[:, 3], m[:, 3], ALU.mult), 3)
                    step(tt(m[:, 7], m[:, 4], m[:, 6], ALU.add), 4)
                    step(tt(m[:, 6], m[:, 7], neg_half[:], ALU.pow), 5)
                    step(tt(quad(tile), quad(tile), m[:, 2].unsqueeze(2).to_broadcast([128, QB, 128]), ALU.subtract), 6)
                    tt(quad(tile), quad(tile), m[:, 6].unsqueeze(2).to_broadcast([128, QB, 128]),
                       ALU.mult).then_inc(ready, 1)
                    norms[0] += 1

                def split_x(job, q):
                    g = group_of(job)
                    n = q % 2
                    src = xg[:, q * QW:(q + 1) * QW]
                    wait(pool, xg_loaded[q], 16 * (g + 1))
                    before = latest(job, "AGG1", (q - 2) % NQ)
                    if present(before):
                        bank_read(pool, before)
                    pool.tensor_tensor(xs[n][0][:], src, one[:].to_broadcast([128, QW]), ALU.mult).then_inc(x_hi, 1)
                    wait(pool, x_hi, nth(g, q))
                    pool.tensor_tensor(xs[n][1][:], src, f32(xs[n][0][:]), ALU.subtract).then_inc(x_split, 1)

                for k in range(NSTEP):
                    for place, wrap, part in due(POOL_PARTS, k):
                        job = (it, parity, place, wrap)
                        stage, q, _ = ORDER[place]
                        g = group_of(job)
                        if not present(job):
                            continue
                        if stage == "AGG1":
                            split_x(job, q)
                        elif stage == "LN1":
                            wait(pool, y1_stats, nth(g, q))
                            normalise(stats1, q, x1[:, q * QW:(q + 1) * QW], x1_ready)
                        elif stage == "KQ":
                            src = x1[:, q * QW:(q + 1) * QW]
                            wait(pool, x1_ready, nth(g, q))
                            wait(pool, row_ready, nth(g, q) - 1)
                            pool.tensor_tensor(quad(row_product[:]), quad(src), spread(query_row[:]),
                                               ALU.mult).then_inc(row_product_ready, 1)
                            wait(pool, y2_stored[q], 16 * g)
                            pool.tensor_tensor(quad(y2[q][:]), quad(src), spread(out_bias[:]),
                                               ALU.add).then_inc(y2_base, 1)
                        elif stage == "SCORE":
                            wait(pool, exp_inverse, nth(g, q))
                            pool.tensor_tensor(quad(prob[:]), quad(expo[:]),
                                               exp_inv[:].unsqueeze(2).to_broadcast([128, QB, 128]),
                                               ALU.mult).then_inc(prob_ready, 1)
                        else:
                            wait(pool, y2_stats, nth(g, q))
                            normalise(stats2, q, y2[q][:], y2_ready)
            iterations(pool, body)

        @block.scalar
        def _(act):
            def copy(dst, src, **kw):
                return act.activation(dst, src, ACT.Copy, **kw)

            def split_weights(j):
                kind, p = LSTM_JOBS[j]
                act.wait_ge(weights_transposed, j + 1)
                for a, b, s in GATE_PARTS:
                    copy(lstm_dst(kind, p, 0)[:, a * 128:b * 128], gate_bank[j % 4][:, a * 128:b * 128],
                         scale=lstm_scale(kind, p, s)).then_inc(weights_hi, 1)

            def side_part(job, part):
                stage, q, _ = ORDER[job[2]]
                bank = side_bank[turn(job)[0]][:]
                g = group_of(job)
                h2 = [tile[:, q * QW:(q + 1) * QW] for tile in state[parity_of(job)]]
                done = act_hi.get(stage)
                if stage in ("AGG1", "AGG2", "XT", "VAL", "PT"):
                    dst = {"AGG1": agg1, "AGG2": agg2, "XT": x1T[q % 2], "VAL": value[q % 2], "PT": probT}[stage]
                    products_done(act, job)
                    copy(dst[0][:], bank).then_inc(done, 1)
                elif stage == "KQ" and part == "shift":
                    wait(act, row_product_ready, nth(g, q))
                    for b in range(QB):
                        ins = copy(bat(row_product, b), bat(row_product, b),
                                   accum_out=row_shift[:, q * QB + b:q * QB + b + 1])
                    ins.then_inc(row_ready, 1)
                elif stage == "KQ":
                    products_done(act, job)
                    act.activation(query[0][:], bank, ACT.Identity, bias=key_bias[:, 0:1]).then_inc(done, 1)
                elif stage in ("PROJ1", "PROJ2"):
                    bank_read(act, job)
                    src, dst = (sum1[:], h1[0][:]) if stage == "PROJ1" else (sum2[:], h2[0])
                    act.activation(dst, src, ACT.Relu).then_inc(done, 1)
                elif part == "exp":
                    wait(act, score_max, nth(g, q))
                    for b in range(QB):
                        ins = act.activation(bat(expo, b), bat(score, b), ACT.Exp, bias=neg_max[:, b:b + 1],
                                             accum_out=exp_sum[:, b:b + 1])
                    ins.then_inc(exp_ready, 1)
                else:
                    bank_read(act, job)
                    copy(refined_parts[0][:], refined[:]).then_inc(done, 1)

            def side_parts(it, parity, k, when):
                for place, wrap, part in due(ACT_PARTS, k, when):
                    if present((it, parity, place, wrap)):
                        side_part((it, parity, place, wrap), part)

            def body(it, parity):
                for k, (p, c, s) in enumerate(STEPS):
                    if has_step(it, k):
                        for gate in (GI, GG, GF, GO):
                            if gate == GF and s == 0:
                                continue
                            wait(act, gate_ready[gate], gate_uses(it, gate, k) + 1)
                            act.activation(packed(gate_tile(it, k, gate), p), packed(gate_bank[gate], p), ACT.Tanh,
                                           bias=gate_bias[:, w_index(p, gate):w_index(p, gate) + 1]
                                           ).then_inc(gate_read[gate], 1)
                    side_parts(it, parity, k, EARLY)
                    if has_step(it, k):
                        wait(act, cell_ready, steps_before(it, k) + 1)
                        act.activation(packed(cell_tanh, p), cell_of(p, c), ACT.Tanh, scale=0.5
                                       ).then_inc(cell_tanh_ready, 1)
                    side_parts(it, parity, k, LATE)
                    for j in weights_due(it, k):
                        split_weights(j)
            iterations(act, body)

        @block.vector
        def _(dve):
            count = [0]

            def done(ins):
                count[0] += 1
                ins.then_inc(setup_dve, 1)

            def own():
                dve.wait_ge(setup_dve, count[0])

            ts, tt, stt, cp = dve.tensor_scalar, dve.tensor_tensor, dve.scalar_tensor_tensor, dve.tensor_copy
            dve.wait_ge(const_loaded, 16 * N_CONST)
            dve.wait_ge(setup_pe, PE_TRANSPOSED)
            done(cp(transposed, side_bank[0][:]))
            done(cp(bq_wide, bq_col.to_broadcast([128, 128])))
            done(cp(bv_wide, bv_col.to_broadcast([128, 128])))
            done(cp(bk_wide, bk_col.to_broadcast([128, 128])))
            assert count[0] == DVE_WIDE
            done(dve.reduce_sum(row_sum, raw_at["adj"], AX.X))
            own()
            done(ts(parent, row_sum, 0.0, gamma_col, ALU.is_gt, ALU.mult))
            own()
            done(ts(keep, parent, -1.0, 1.0, ALU.mult, ALU.add))
            own()
            dve.wait_ge(setup_pool, 7)
            done(ts(diagonal, ident[:], keep, None, ALU.mult))
            own()
            done(stt(out=mixing, in0=raw_at["adj"], scalar=parent, in1=diagonal, op0=ALU.mult, op1=ALU.add))
            assert count[0] == DVE_AP
            dve.wait_ge(setup_pe, PE_MIXT)
            done(cp(mixT_f, side_bank[3][:, 0:128]))
            assert count[0] == DVE_MIXT
            dve.wait_ge(setup_pe, PE_SHIFTS)
            done(tt(shift_rows, side_bank[2][:, 0:128], raw_at["bo"], ALU.add))
            assert count[0] == DVE_SHIFT_ROWS
            dve.wait_ge(lstm_loaded, 64)
            done(tt(bih_rows, bih_rows, bhh_rows, ALU.add))
            assert count[0] == DVE_BIAS_ROWS
            done(ts(key_bias[:], side_bank[2][:, 128:129], SCALE, None, ALU.mult))
            dve.wait_ge(setup_pe, PE_FOLDED)
            done(ts(query_row[:], side_bank[3][:, 128:256], SCALE, None, ALU.mult))
            done(ts(row_const, side_bank[2][:, 130:131], SCALE, None, ALU.mult))
            dve.wait_ge(setup_pe, PE_FOLDED)
            done(cp(bias1[:], side_bank[1][:, 0:128]))
            done(cp(bias2[:], side_bank[1][:, 128:256]))
            done(ts(kq[0][:], side_bank[1][:, 256:384], SCALE, None, ALU.mult))
            done(cp(vo[0][:], side_bank[1][:, 384:512]))
            own()
            done(cp(adjT[0][:], adjT_f))
            done(cp(wg0[0][:], raw_at["Wg0"]))
            done(cp(wg1[0][:], raw_at["Wg1"]))
            done(cp(mixT[0][:], mixT_f))
            done(ts(mask_bias[:], raw_at["adj"], 0.0, MASKED, ALU.is_equal, ALU.mult))
            own()
            done(stt(out=kq[1][:], in0=side_bank[1][:, 256:384], scalar=SCALE, in1=f32(kq[0][:]),
                     op0=ALU.mult, op1=ALU.subtract))
            done(tt(vo[1][:], side_bank[1][:, 384:512], f32(vo[0][:]), ALU.subtract))
            done(tt(adjT[1][:], adjT_f, f32(adjT[0][:]), ALU.subtract))
            done(tt(wg0[1][:], raw_at["Wg0"], f32(wg0[0][:]), ALU.subtract))
            done(tt(wg1[1][:], raw_at["Wg1"], f32(wg1[0][:]), ALU.subtract))
            done(tt(mixT[1][:], mixT_f, f32(mixT[0][:]), ALU.subtract))
            done(stt(out=mask_bias[:], in0=raw_at["adj"], scalar=alpha_col, in1=mask_bias[:], op0=ALU.mult, op1=ALU.add))
            own()
            done(ts(mask_bias[:], mask_bias[:], row_const, None, ALU.add))
            dve.wait_ge(setup_pe, PE_OUTBIAS)
            done(cp(out_bias[:], gate_bank[0][:, 0:128]))
            dve.wait_ge(setup_pe, PE_BIAS)
            done(ts(gate_bias[:], gate_bank[1][:, 0:16], 0.5, None, ALU.mult))
            own()
            done(cp(gate_bias[:, 2:16:4], gate_bank[1][:, 2:16:4]))
            assert count[0] == SETUP_DVE, count[0]

            def split_weights(j):
                kind, p = LSTM_JOBS[j]
                dve.wait_ge(weights_hi, 3 * (j + 1))
                for a, b, s in GATE_PARTS:
                    cols = slice(a * 128, b * 128)
                    stt(out=lstm_dst(kind, p, 1)[:, cols], in0=gate_bank[j % 4][:, cols],
                        scalar=lstm_scale(kind, p, s), in1=f32(lstm_dst(kind, p, 0)[:, cols]),
                        op0=ALU.mult, op1=ALU.subtract).then_inc(weights_lo, 1)

            def side_part(job, part):
                stage, q, _ = ORDER[job[2]]
                number, _ = turn(job)
                bank = side_bank[number][:]
                read = side_read[number]
                g = group_of(job)
                h2 = [tile[:, q * QW:(q + 1) * QW] for tile in state[parity_of(job)]]
                if stage in ("AGG1", "AGG2", "XT", "VAL", "PT"):
                    dst = {"AGG1": agg1, "AGG2": agg2, "XT": x1T[q % 2], "VAL": value[q % 2], "PT": probT}[stage]
                    wait(dve, act_hi[stage], nth(g, q))
                    tt(dst[1][:], bank, f32(dst[0][:]), ALU.subtract).then_inc(read, 1)
                elif stage == "KQ":
                    wait(dve, act_hi[stage], nth(g, q))
                    stt(out=query[1][:], in0=bank, scalar=key_bias[:, 0:1], in1=f32(query[0][:]),
                        op0=ALU.add, op1=ALU.subtract).then_inc(read, 1)
                elif stage in ("PROJ1", "PROJ2"):
                    total, const = (sum1, bias1) if stage == "PROJ1" else (sum2, bias2)
                    if part == "sum":
                        products_done(dve, job)
                        tt(quad(total[:]), quad(bank), spread(const[:]), ALU.add).then_inc(read, 1)
                    else:
                        hi, lo = ((h1[0][:], h1[1][:]) if stage == "PROJ1"
                                  else (h2[0], h2[1]))
                        wait(dve, act_hi[stage], nth(g, q))
                        stt(out=lo, in0=total[:], scalar=0.0, in1=f32(hi), op0=ALU.max, op1=ALU.subtract
                            ).then_inc(h1_split if stage == "PROJ1" else h2_split, 1)
                elif stage == "LN1":
                    dst = x1[:, q * QW:(q + 1) * QW]
                    wait(dve, x1_loaded[q], 16 * (g + 1))
                    products_done(dve, job)
                    stt(out=dst, in0=bank, scalar=0.5, in1=dst, op0=ALU.mult, op1=ALU.add).then_inc(read, 1)
                    bank_read(dve, job)
                    for b in range(QB):
                        ins = dve.bn_stats(quad_stats(stats1, q, b), bat(dst, b))
                    ins.then_inc(y1_stats, 1)
                elif stage == "SCORE" and part == "sum":
                    products_done(dve, job)
                    wait(dve, row_ready, nth(g, q))
                    for b in range(QB):
                        ins = stt(out=bat(score, b), in0=bat(bank, b), scalar=row_shift[:, q * QB + b:q * QB + b + 1],
                                  in1=mask_bias[:], op0=ALU.add, op1=ALU.add)
                    ins.then_inc(read, 1)
                    bank_read(dve, job)
                    dve.tensor_reduce(neg_max[:], quad(score[:]), AX.X, ALU.max, negate=True).then_inc(score_max, 1)
                elif stage == "SCORE" and part == "inv":
                    wait(dve, exp_ready, nth(g, q))
                    dve.reciprocal(exp_inv[:], exp_sum[:]).then_inc(exp_inverse, 1)
                elif stage == "PV" and part == "sum":
                    products_done(dve, job)
                    tt(refined[:], bank, x1[:, q * QW:(q + 1) * QW], ALU.add).then_inc(read, 1)
                elif stage == "PV":
                    wait(dve, act_hi[stage], nth(g, q))
                    tt(refined_parts[1][:], refined[:], f32(refined_parts[0][:]), ALU.subtract
                       ).then_inc(refined_split, 1)
                else:
                    dst = y2[q]
                    products_done(dve, job)
                    wait(dve, y2_base, nth(g, q))
                    tt(dst[:], bank, dst[:], ALU.add).then_inc(read, 1)
                    bank_read(dve, job)
                    for b in range(QB):
                        ins = dve.bn_stats(quad_stats(stats2, q, b), bat(dst, b))
                    ins.then_inc(y2_stats, 1)

            def new_cell(it, k):
                p, c, s = STEPS[k]
                ti, tf, tg = (packed(gate_tile(it, k, g), p) for g in (GI, GF, GG))
                old = cell_of(p, c)
                before = steps_before(it, k, lambda step: step[2] > 0) * 2
                wait(dve, gate_read[GG], gate_uses(it, GG, k) + 1)
                if s == 0:
                    stt(out=old, in0=ti, scalar=1.0, in1=tg, op0=ALU.add, op1=ALU.mult).then_inc(cell_ready, 1)
                    return
                stt(out=ti, in0=ti, scalar=1.0, in1=tg, op0=ALU.add, op1=ALU.mult).then_inc(cell_term, 1)
                wait(dve, gate_read[GF], gate_uses(it, GF, k) + 1)
                stt(out=tf, in0=tf, scalar=1.0, in1=old, op0=ALU.add, op1=ALU.mult).then_inc(cell_term, 1)
                wait(dve, cell_term, before + 2)
                stt(out=old, in0=tf, scalar=0.5, in1=ti, op0=ALU.mult, op1=ALU.add).then_inc(cell_ready, 1)

            def new_hidden(it, k, parity):
                p, c, s = STEPS[k]
                to = packed(gate_tile(it, k, GO), p)
                parity = (parity - (p == 4)) % 2
                kept = s == p - 1
                full = window(final[parity], p, c, s) if kept else packed(fresh, p)
                count = steps_before(it, k) + 1
                wait(dve, gate_read[GO], gate_uses(it, GO, k) + 1)
                wait(dve, cell_tanh_ready, count)
                stt(out=full, in0=to, scalar=1.0, in1=packed(cell_tanh, p), op0=ALU.add, op1=ALU.mult
                    ).then_inc(h_full, 1)
                if not is_split((p, c, s)):
                    return
                hi, lo = ((window(t, p, c, s) for t in state[parity]) if kept
                          else (packed(t, p) for t in hidden[lane(p, c)]))
                wait(dve, h_full, count)
                cp(hi, full).then_inc(h_hi, 1)
                wait(dve, h_hi, splits_before(it, k) + 1)
                tt(lo, full, f32(hi), ALU.subtract).then_inc(h_split, 1)

            def side_parts(it, parity, k, when):
                for place, wrap, part in due(DVE_PARTS, k, when):
                    if present((it, parity, place, wrap)):
                        side_part((it, parity, place, wrap), part)

            def body(it, parity):
                for k in range(NSTEP):
                    if has_step(it, k):
                        new_cell(it, k)
                    side_parts(it, parity, k, EARLY)
                    if has_step(it, k):
                        new_hidden(it, k, parity)
                    side_parts(it, parity, k, LATE)
                    for j in weights_due(it, k):
                        split_weights(j)
            iterations(dve, body)

        @block.tensor
        def _(pe):
            def mm(dst, lhsT, rhs, start, stop):
                return nc.tensor.matmul(dst, lhsT, rhs, start=start, stop=stop)

            pe.wait_ge(const_loaded, 16 * N_CONST)
            pe.wait_ge(setup_pool, 7)
            for i, name in enumerate(("adj", "Wq", "Wk", "Wv")):
                ins = nc.tensor.transpose(bat(side_bank[0], i), raw_at[name], ident[:])
            ins.then_inc(setup_pe, 1)
            pe.wait_ge(setup_dve, DVE_WIDE)
            mm(side_bank[3][:, 128:256], bk_wide, wqT, True, True)
            mm(side_bank[1][:, 0:128], adjT_f, raw_at["bg0"], True, True)
            mm(side_bank[1][:, 128:256], raw_at["bg1"], adjT_f, True, True)
            mm(side_bank[1][:, 256:384], wqT, wkT, True, True)
            mm(side_bank[1][:, 384:512], wvT, raw_at["Wo"], True, True).then_inc(setup_pe, 1)
            mm(side_bank[2][:, 0:128], bv_wide, raw_at["Wo"], True, True)
            mm(side_bank[2][:, 128:129], wkT, bq_col, True, True)
            mm(side_bank[2][:, 130:131], bq_wide, bk_col, True, True).then_inc(setup_pe, 1)
            pe.wait_ge(setup_dve, DVE_AP)
            nc.tensor.transpose(side_bank[3][:, 0:128], mixing, ident[:]).then_inc(setup_pe, 1)
            pe.wait_ge(setup_dve, DVE_SHIFT_ROWS)
            mm(gate_bank[0][:, 0:128], mixT_f, shift_rows, True, True).then_inc(setup_pe, 1)
            pe.wait_ge(setup_dve, DVE_BIAS_ROWS)
            nc.tensor.transpose(gate_bank[1][:, 0:16], bih_rows, ident[0:16, 0:16]).then_inc(setup_pe, 1)
            pe.wait_ge(setup_dve, SETUP_DVE)

            def transpose_weights(j):
                kind, p = LSTM_JOBS[j]
                if j >= 4:
                    pe.wait_ge(weights_lo, 3 * (j - 3))
                src = raw_ih if kind == "ih" else raw_hh
                for gate in range(4):
                    ins = nc.tensor.transpose(bat(gate_bank[j % 4], gate), bat(src, w_index(p, gate)), ident[:])
                ins.then_inc(weights_transposed, 1)

            def three(dst, a, b, start, stop):
                mm(dst, a[0], b[0], start, False)
                mm(dst, a[0], b[1], False, False)
                return mm(dst, a[1], b[0], False, stop)

            def both(pair, cut):
                return [cut(t) for t in pair]

            def side_job(job):
                stage, q, _ = ORDER[job[2]]
                number, before = turn(job)
                bank = side_bank[number]
                g = group_of(job)
                wait(pe, side_read[number], before)

                def per_batch(a, b_of):
                    for i in range(QB):
                        ins = three(bat(bank, i), both(a, lambda t: bat(t, i)), b_of(i), True, True)
                    return ins

                if stage == "AGG1":
                    wait(pe, x_split, nth(g, q))
                    ins = per_batch(xs[q % 2], lambda i: both(adjT, lambda t: t[:]))
                elif stage == "PROJ1":
                    bank_read(pe, latest(job, "AGG1", q))
                    ins = per_batch(agg1, lambda i: both(wg0, lambda t: t[:]))
                elif stage == "AGG2":
                    wait(pe, h1_split, nth(g, q))
                    ins = per_batch(h1, lambda i: both(adjT, lambda t: t[:]))
                elif stage == "PROJ2":
                    bank_read(pe, latest(job, "AGG2", q))
                    ins = three(bank[:], both(wg1, lambda t: t[:]), both(agg2, lambda t: t[:]), True, True)
                elif stage == "LN1":
                    wait(pe, h_full, steps_before(g + 1, STEPS.index((4, 0, 3))) + 1)
                    for i in range(QB):
                        ins = nc.tensor.transpose(bat(bank, i), bat(final[parity_of(job)], q * QB + i), ident[:])
                elif stage == "XT":
                    wait(pe, x1_ready, nth(g, q))
                    for i in range(QB):
                        ins = nc.tensor.transpose(bat(bank, i), bat(x1, q * QB + i), ident[:])
                elif stage == "KQ":
                    bank_read(pe, latest(job, "XT", q))
                    ins = three(bank[:], both(kq, lambda t: t[:]), both(x1T[q % 2], lambda t: t[:]), True, True)
                elif stage == "VAL":
                    ins = per_batch(x1T[q % 2], lambda i: both(vo, lambda t: t[:]))
                elif stage == "SCORE":
                    bank_read(pe, latest(job, "KQ", q))
                    ins = per_batch(query, lambda i: both(x1T[q % 2], lambda t: bat(t, i)))
                elif stage == "PT":
                    wait(pe, prob_ready, nth(g, q))
                    for i in range(QB):
                        ins = nc.tensor.transpose(bat(bank, i), bat(prob, i), ident[:])
                elif stage == "PV":
                    needed = {turn(ref)[0]: ref for ref in sorted(
                        (latest(job, "PT", q), latest(job, "VAL", q)), key=lambda ref: (-ref[3], ref[2]))}
                    for at, ref in needed.items():
                        if at != number:
                            bank_read(pe, ref)
                    ins = per_batch(probT, lambda i: both(value[q % 2], lambda t: bat(t, i)))
                else:
                    wait(pe, refined_split, nth(g, q))
                    ins = three(bank[:], both(mixT, lambda t: t[:]), both(refined_parts, lambda t: t[:]), True, True)
                ins.then_inc(side_ready[number], 1)

            def lstm_step(it, k, parity):
                p, c, s = STEPS[k]
                used = [g for g in (GI, GG, GF, GO) if g != GF or s > 0]
                own_state = state[(parity - (p == 4)) % 2]
                if p == 1:
                    wait(pe, h2_split, nth(it, c))
                elif p == 4:
                    wait(pe, h_split, splits_before(it, 0))
                else:
                    end = (1, 2 * c + 1, 0) if p == 2 else (2, c, 1)
                    wait(pe, h_split, splits_before(it, STEPS.index(end)) + 1)
                inputs = both(own_state, lambda t: window(t, p, c, s))
                for gate in used:
                    at = w_index(p, gate)
                    wait(pe, gate_read[gate], gate_uses(it, gate, k))
                    ins = three(packed(gate_bank[gate], p), both(wih, lambda t: bat(t, at)), inputs, True, s == 0)
                    if s == 0:
                        ins.then_inc(gate_ready[gate], 1)
                if s > 0:
                    wait(pe, h_split, splits_before(it, STEPS.index((p, c, s - 1))) + 1)
                    for gate in used:
                        at = (p - 2) * 4 + gate
                        three(packed(gate_bank[gate], p), both(whh, lambda t: bat(t, at)),
                              both(hidden[lane(p, c)], lambda t: packed(t, p)), False, True).then_inc(gate_ready[gate], 1)

            def body(it, parity):
                for k in range(NSTEP):
                    if has_step(it, k):
                        lstm_step(it, k, parity)
                    for place in range(FIRST[k], FIRST[k + 1]):
                        if present((it, parity, place, 0)):
                            side_job((it, parity, place, 0))
                    for j in weights_due(it, k):
                        transpose_weights(j)
                if isinstance(it, int) and it == -1:
                    pe.wait_ge(weights_lo, 3 * len(LSTM_JOBS))
            iterations(pe, body)


_INS = ['x', 'adj', 'L0_gnn_Wg0', 'L0_gnn_bg0', 'L0_gnn_Wg1', 'L0_gnn_bg1', 'L0_gnn_Wih', 'L0_gnn_Whh',
        'L0_gnn_bih', 'L0_gnn_bhh', 'L1_gnn_Wq', 'L1_gnn_bq', 'L1_gnn_Wk', 'L1_gnn_bk', 'L1_gnn_Wv',
        'L1_gnn_bv', 'L1_gnn_Wo', 'L1_gnn_bo', 'L1_gnn_alpha', 'L1_gnn_gamma']


def kernel(**inputs):
    import numpy as _np
    import concourse.bacc as _bacc
    from concourse import mybir as _mybir
    from concourse.bass_utils import run_bass_kernel_spmd as _run

    nc = _bacc.Bacc("TRN2", target_bir_lowering=False, num_devices=1)
    arrays, args = {}, []
    for name in _INS:
        a = _np.ascontiguousarray(inputs[name]).reshape(_np.shape(inputs[name]) or (1,))
        arrays[f"in_{name}_dram"] = a
        args.append(nc.dram_tensor(f"in_{name}_dram", a.shape, _mybir.dt.from_np(a.dtype), kind="ExternalInput").ap())
    args.append(nc.dram_tensor("out_0_dram", (NB, T, D), F32, kind="ExternalOutput").ap())
    graph_resnorm_kernel(nc, *args)
    r = _run(nc, [arrays], core_ids=[0])
    return r.results[0]["out_0_dram"]
```

```python
from contextlib import ExitStack

import concourse.bass as bass
from concourse import mybir

F32 = mybir.dt.float32
F32R = mybir.dt.float32r
ALU = mybir.AluOpType
ACT = mybir.ActivationFunctionType
AX = mybir.AxisListType

NB, T, D = 128, 128, 128
GB, QB = 16, 4
NG, NQ = NB // GB, GB // QB
QW = QB * T
GW = GB * T
EPS = 1e-5
MASKED = -1e30
SCALE = float(D) ** -0.5


GI, GF, GG, GO = range(4)

STEPS = ([(1, 0, 0), (4, 0, 0), (1, 1, 0), (4, 0, 1), (1, 2, 0), (4, 0, 2), (1, 3, 0), (4, 0, 3)]
         + [(2, c, s) for s in range(2) for c in range(2)]
         + [(3, c, s) for s in range(3) for c in range(2)])
NCHUNK = {1: 4, 2: 2, 3: 2, 4: 1}
NSTEP = len(STEPS)

FILL = [
    [("PROJ2", 2, 0), ("VAL", 0, 2), ("PT", 0, 2)],
    [("AGG2", 3, 0), ("LN1", 3, 2)],
    [("SCORE", 1, 2), ("XT", 2, 2)],
    [("PROJ2", 3, 0), ("VAL", 1, 2)],
    [("KQ", 2, 2), ("PV", 0, 2), ("AGG1", 0, -1)],
    [("PT", 1, 2), ("SCORE", 2, 2)],
    [("XT", 3, 2), ("OUT", 0, 2)],
    [("PROJ1", 0, -1), ("PV", 1, 2), ("VAL", 2, 2)],
    [("KQ", 3, 2), ("AGG1", 1, -1), ("LN1", 0, 1), ("AGG2", 0, -1)],
    [("VAL", 3, 2), ("PROJ1", 1, -1), ("PT", 2, 2)],
    [("SCORE", 3, 2)],
    [("OUT", 1, 2), ("XT", 0, 1)],
    [("PROJ2", 0, -1), ("AGG1", 2, -1), ("PV", 2, 2), ("AGG2", 1, -1)],
    [("KQ", 0, 1), ("LN1", 1, 1)],
    [("PROJ1", 2, -1), ("PT", 3, 2)],
    [("AGG1", 3, -1), ("PROJ2", 1, -1), ("OUT", 2, 2), ("PV", 3, 2)],
    [("XT", 1, 1), ("SCORE", 0, 1), ("AGG2", 2, -1)],
    [("OUT", 3, 2), ("KQ", 1, 1), ("LN1", 2, 1), ("PROJ1", 3, -1)],
]
START = [
    [], [], [], [],
    [("AGG1", 0, -1)],
    [], [],
    [("PROJ1", 0, -1)],
    [("AGG1", 1, -1), ("AGG2", 0, -1)],
    [("PROJ1", 1, -1)],
    [], [],
    [("PROJ2", 0, -1), ("AGG1", 2, -1), ("AGG2", 1, -1)],
    [("PROJ1", 2, -1)],
    [],
    [("AGG1", 3, -1), ("PROJ2", 1, -1)],
    [("AGG2", 2, -1)],
    [("PROJ1", 3, -1)],
]
DRAIN = [
    [("VAL", 0, 2), ("PT", 0, 2)],
    [("LN1", 3, 2)],
    [("SCORE", 1, 2), ("XT", 2, 2)],
    [("PV", 0, 2), ("VAL", 1, 2)],
    [("KQ", 2, 2)],
    [("PT", 1, 2)],
    [("VAL", 2, 2), ("XT", 3, 2), ("OUT", 0, 2)],
    [("PV", 1, 2), ("SCORE", 2, 2)],
    [("KQ", 3, 2), ("LN1", 0, 1)],
    [("VAL", 3, 2), ("OUT", 1, 2), ("PT", 2, 2)],
    [("SCORE", 3, 2), ("XT", 0, 1)],
    [("PV", 2, 2), ("LN1", 1, 1)],
    [("KQ", 0, 1), ("PT", 3, 2)],
    [("OUT", 2, 2), ("VAL", 0, 1), ("PV", 3, 2)],
    [("SCORE", 0, 1), ("XT", 1, 1)],
    [("OUT", 3, 2), ("LN1", 2, 1), ("KQ", 1, 1)],
    [("PT", 0, 1), ("VAL", 1, 1), ("SCORE", 1, 1)],
    [("PV", 0, 1), ("XT", 2, 1), ("LN1", 3, 1)],
]
END = [
    [("OUT", 0, 2), ("KQ", 2, 2), ("PT", 1, 2), ("VAL", 2, 2)],
    [("PV", 1, 2), ("SCORE", 2, 2), ("XT", 3, 2)],
    [("KQ", 3, 2)],
    [("OUT", 1, 2), ("PT", 2, 2), ("SCORE", 3, 2), ("VAL", 3, 2)],
    [("PV", 2, 2)],
    [("PT", 3, 2)],
    [("OUT", 2, 2), ("PV", 3, 2)],
    [("OUT", 3, 2)],
    [], [], [], [], [], [], [], [], [], [],
]
LOOP_FIRST, LOOP_ROUNDS = 3, 2


def fill(it):
    return {-1: START, NG: DRAIN, NG + 1: END}.get(it, FILL)


def order(it):
    return [job for slot in fill(it) for job in slot]


EARLY, LATE = range(2)
ACT_PARTS = {
    "AGG1": [("hi", 0, LATE)],
    "PROJ1": [("hi", 1, EARLY)],
    "AGG2": [("hi", 0, LATE)],
    "PROJ2": [("hi", 1, EARLY)],
    "XT": [("hi", 0, LATE)],
    "KQ": [("hi", 0, LATE), ("shift", 1, LATE)],
    "VAL": [("hi", 0, LATE)],
    "SCORE": [("exp", 1, EARLY)],
    "PT": [("hi", 0, LATE)],
    "PV": [("hi", 1, EARLY)],
}
DVE_PARTS = {
    "AGG1": [("lo", 0, LATE)],
    "PROJ1": [("sum", 0, EARLY), ("lo", 1, EARLY)],
    "AGG2": [("lo", 0, LATE)],
    "PROJ2": [("sum", 0, EARLY), ("lo", 1, EARLY)],
    "LN1": [("sum", 1, EARLY)],
    "XT": [("lo", 0, LATE)],
    "KQ": [("prepare", 0, LATE), ("lo", 0, LATE)],
    "VAL": [("lo", 0, LATE)],
    "SCORE": [("sum", 0, LATE), ("inv", 1, LATE)],
    "PT": [("lo", 0, LATE)],
    "PV": [("sum", 0, EARLY), ("lo", 1, EARLY)],
    "OUT": [("sum", 0, EARLY)],
}
POOL_PARTS = {
    "AGG1": [("split", -3, LATE)],
    "LN1": [("norm", 0, LATE)],
    "KQ": [("prepare", -1, LATE)],
    "SCORE": [("norm", 1, LATE)],
    "OUT": [("norm", 2, LATE)],
}
SP_PARTS = {
    "AGG1": [("load", -4, LATE)],
    "OUT": [("load", 1, LATE), ("store", 2, LATE)],
}


def due(parts, it, k, when=LATE):
    found = []
    for later in range(3, -5, -1):
        step, wrap = (k - later) % NSTEP, -((k - later) // NSTEP)
        slots = fill(it - wrap if isinstance(it, int) else None)
        first = sum(len(slot) for slot in slots[:step])
        for n, (stage, _, _) in enumerate(slots[step]):
            found += [(first + n, wrap, part) for part, steps, at in parts.get(stage, [])
                      if steps == later and at == when]
    return found


def graph_resnorm_kernel(nc, x, adj, Wg0, bg0, Wg1, bg1, Wih, Whh, bih, bhh,
                         Wq, bq, Wk, bk, Wv, bv, Wo, bo, alpha, gamma, out):
    with ExitStack() as ctx:
        def sb(name, cols, dt=F32, rows=128):
            return ctx.enter_context(nc.sbuf_tensor(name, [rows, cols], dt))

        def sem(name):
            return ctx.enter_context(nc.semaphore(name))

        def quad(ap):
            return ap.rearrange("p (b t) -> p b t", b=QB)

        def spread(ap):
            return ap.unsqueeze(1).to_broadcast([128, QB, 128])

        gate_bank = [ctx.enter_context(nc.psum_tensor(f"gate_bank{i}", [128, 512], F32)) for i in range(4)]
        side_bank = [ctx.enter_context(nc.psum_tensor(f"side_bank{i}", [128, 512], F32)) for i in range(4)]

        ident = sb("ident", 128)
        adjT = [sb(f"adjT_{h}", 128, F32R) for h in ("hi", "lo")]
        wg0 = [sb(f"wg0_{h}", 128, F32R) for h in ("hi", "lo")]
        wg1 = [sb(f"wg1_{h}", 128, F32R) for h in ("hi", "lo")]
        kq = [sb(f"kq_{h}", 128, F32R) for h in ("hi", "lo")]
        vo = [sb(f"vo_{h}", 128, F32R) for h in ("hi", "lo")]
        query_row = sb("query_row", 128)
        mixT = [sb(f"mixT_{h}", 128, F32R) for h in ("hi", "lo")]
        wih = [sb(f"wih_{h}", 16 * 128, F32R) for h in ("hi", "lo")]
        whh = [sb(f"whh_{h}", 12 * 128, F32R) for h in ("hi", "lo")]
        gate_bias = sb("gate_bias", 16)
        bias1 = sb("bias1", 128)
        bias2 = sb("bias2", 128)
        key_bias = sb("key_bias", 1)
        mask_bias = sb("mask_bias", 128)
        out_bias = sb("out_bias", 128)
        half = sb("half", 8)
        one = sb("one", 1)
        inv_d = sb("inv_d", 4)
        eps = sb("eps", 4)
        neg_half = sb("neg_half", 4)

        xg = sb("xg", GW)
        xs = [[sb(f"xs{n}_{h}", QW, F32R) for h in ("hi", "lo")] for n in range(2)]
        agg1 = [sb(f"agg1_{h}", QW, F32R) for h in ("hi", "lo")]
        sum1 = sb("sum1", QW)
        h1 = [sb(f"h1_{h}", QW, F32R) for h in ("hi", "lo")]
        agg2 = [sb(f"agg2_{h}", QW, F32R) for h in ("hi", "lo")]
        sum2 = sb("sum2", QW)

        state = [[sb(f"state{n}_{h}", GW, F32R) for h in ("hi", "lo")] for n in range(2)]
        gates = sb("gates", 2 * 4 * 512)
        final = [sb(f"final{n}", GW) for n in range(2)]
        cell = sb("cell", 2 * 512)
        cell_tanh = sb("cell_tanh", 512)
        fresh = sb("fresh", 512)
        hidden = [[sb(f"hidden{n}_{h}", 512, F32R) for h in ("hi", "lo")] for n in range(2)]

        x1 = sb("x1", GW)
        stats1 = sb("stats1", NQ * QB * 6)
        stats2 = sb("stats2", NQ * QB * 6)
        moments = sb("moments", 8 * 4)
        x1T = [[sb(f"x1T{n}_{h}", QW, F32R) for h in ("hi", "lo")] for n in range(2)]
        query = [sb(f"query_{h}", QW, F32R) for h in ("hi", "lo")]
        value = [[sb(f"value{n}_{h}", QW, F32R) for h in ("hi", "lo")] for n in range(2)]
        row_product = sb("row_product", QW)
        row_shift = sb("row_shift", NQ * QB)
        score = sb("score", QW)
        neg_max = sb("neg_max", QB)
        expo = sb("expo", QW)
        exp_sum = sb("exp_sum", QB)
        exp_inv = sb("exp_inv", QB)
        prob = sb("prob", QW)
        probT = [sb(f"probT_{h}", QW, F32R) for h in ("hi", "lo")]
        refined = sb("refined", QW)
        refined_parts = [sb(f"refined_{h}", QW, F32R) for h in ("hi", "lo")]
        y2 = [sb(f"y2_{n}", QW) for n in range(NQ)]

        const_loaded = sem("const_loaded")
        lstm_loaded = sem("lstm_loaded")
        setup_pe = sem("setup_pe")
        weights_transposed = sem("weights_transposed")
        weights_hi = sem("weights_hi")
        weights_lo = sem("weights_lo")
        setup_dve = sem("setup_dve")
        setup_pool = sem("setup_pool")
        xg_loaded = [sem(f"xg_loaded{q}") for q in range(NQ)]
        x1_loaded = [sem(f"x1_loaded{q}") for q in range(NQ)]
        y2_stored = [sem(f"y2_stored{q}") for q in range(NQ)]
        gate_ready = [sem(f"gate_ready{i}") for i in range(4)]
        gate_read = [sem(f"gate_read{i}") for i in range(4)]
        side_ready = [sem(f"side_ready{i}") for i in range(4)]
        side_read = [sem(f"side_read{i}") for i in range(4)]
        cell_term = sem("cell_term")
        cell_ready = sem("cell_ready")
        cell_tanh_ready = sem("cell_tanh_ready")
        h_full = sem("h_full")
        h_hi = sem("h_hi")
        h_split = sem("h_split")
        act_hi = {s: sem(f"hi_{s}") for s in ("AGG1", "PROJ1", "AGG2", "PROJ2", "XT", "KQ", "VAL", "PT", "PV")}
        x_hi = sem("x_hi")
        x_split = sem("x_split")
        pool_step = sem("pool_step")
        h1_split = sem("h1_split")
        h2_split = sem("h2_split")
        y1_stats = sem("y1_stats")
        x1_ready = sem("x1_ready")
        row_product_ready = sem("row_product_ready")
        row_ready = sem("row_ready")
        y2_base = sem("y2_base")
        score_max = sem("score_max")
        exp_ready = sem("exp_ready")
        exp_inverse = sem("exp_inverse")
        prob_ready = sem("prob_ready")
        refined_split = sem("refined_split")
        y2_stats = sem("y2_stats")
        y2_ready = sem("y2_ready")

        def f32(ap):
            return ap.bitcast(F32)

        def wait(eng, s, value):
            if not isinstance(value, int) or value > 0:
                eng.wait_ge(s, value)

        def nth(group, q):
            return group * NQ + (q + 1)

        def counted(it, f):
            if isinstance(it, int):
                return f(it)
            first = f(LOOP_FIRST)
            rate = f(LOOP_FIRST + 1) - first
            assert all(f(LOOP_FIRST + n) == first + n * rate for n in range(2 * LOOP_ROUNDS))
            return it * rate + (first - LOOP_FIRST * rate)

        def quad_stats(stats, q, b):
            at = (q * QB + b) * 6
            return stats[:, at:at + 6]

        def bat(ap, b):
            return ap[:, b * 128:(b + 1) * 128]

        def entry(job):
            it, _, place, wrap = job
            return order(it - wrap if isinstance(it, int) else None)[place]

        def group_of(job):
            it, _, _, wrap = job
            return it - (wrap + entry(job)[2])

        def parity_of(job):
            _, parity, _, wrap = job
            return (parity - wrap - entry(job)[2]) % 2

        def in_range(group):
            return not isinstance(group, int) or 0 <= group < NG

        def present(job):
            return in_range(group_of(job))

        def find(job, stage, q, groups_back=0):
            it, parity, _, wrap = job
            behind = wrap + entry(job)[2] + groups_back
            for w in range(-1, 4):
                jobs = order(it - w if isinstance(it, int) else None)
                if (stage, q, behind - w) in jobs:
                    return it, parity, jobs.index((stage, q, behind - w)), w
            return None

        def jobs_before(it, place):
            return sum(1 for t in range(-1, it + 1) for n, (_, _, lag) in enumerate(order(t))
                       if 0 <= t - lag < NG and (t < it or n < place))

        def draining(job):
            it, _, _, wrap = job
            return isinstance(it, int) and it - wrap >= NG

        def turn(job):
            it, _, place, wrap = job
            bank = jobs_before((it if isinstance(it, int) else LOOP_FIRST) - wrap, place) % 4
            return bank, counted(it, lambda t: jobs_before(t - wrap, place) // 4)

        def products_done(eng, job):
            bank, before = turn(job)
            wait(eng, side_ready[bank], before + 1)

        def bank_read(eng, job):
            bank, before = turn(job)
            wait(eng, side_read[bank], before + 1)

        def step_group(it, k):
            return it - (STEPS[k][0] == 4)

        def has_step(it, k):
            return in_range(step_group(it, k))

        def steps_before(it, k, kind=lambda step: True):
            return counted(it, lambda t: sum(
                1 for u in range(0, t + 1) for n, step in enumerate(STEPS)
                if kind(step) and has_step(u, n) and (u < t or n < k)))

        def is_split(step):
            return step != (4, 0, 3)

        def splits_before(it, k):
            return steps_before(it, k, is_split)

        def gate_uses(it, gate, k):
            return steps_before(it, k, lambda step: gate != GF or step[2] > 0)

        def lane(p, chunk):
            return {1: 0, 4: 1}.get(p, chunk)

        def cell_of(p, chunk):
            return packed(cell[:, lane(p, chunk) * 512:(lane(p, chunk) + 1) * 512], p)

        def prepare(eng, job):
            q, g = entry(job)[1], group_of(job)
            src = x1[:, q * QW:(q + 1) * QW]
            wait(eng, x1_ready, nth(g, q))
            wait(eng, row_ready, nth(g, q) - 1)
            eng.tensor_tensor(quad(row_product[:]), quad(src), spread(query_row[:]),
                              ALU.mult).then_inc(row_product_ready, 1)
            if draining(job):
                wait(eng, y2_base, nth(g, q) - 1)
            wait(eng, y2_stored[q], 16 * g)
            eng.tensor_tensor(quad(y2[q][:]), quad(src), spread(out_bias[:]), ALU.add).then_inc(y2_base, 1)

        def window(tile, p, chunk, s):
            nb = GB // NCHUNK[p]
            nw = T // p
            return tile[:, chunk * nb * T:(chunk + 1) * nb * T].rearrange(
                "h (b t) -> h b t", b=nb)[:, :, s:s + p * (nw - 1) + 1:p]

        def packed(tile, p):
            nb = GB // NCHUNK[p]
            nw = T // p
            return tile[:, 0:nb * nw].rearrange("h (b w) -> h b w", b=nb)

        def gate_tile(it, k, gate):
            turn_of = steps_before(it if isinstance(it, int) else LOOP_FIRST, k) % 2
            at = (turn_of * 4 + gate) * 512
            return gates[:, at:at + 512]

        def w_index(p, gate):
            return (p - 1) * 4 + gate

        raw_ih, raw_hh = final
        raw = gates
        raw_at = {n: raw[:, i * 128:(i + 1) * 128] for i, n in enumerate(
            ("adj", "Wq", "Wk", "Wv", "Wo", "Wg0", "Wg1", "bg0", "bg1", "bo"))}
        transposed = raw[:, 1280:1792]
        adjT_f, wqT, wkT, wvT = (transposed[:, i * 128:(i + 1) * 128] for i in range(4))
        bq_wide = raw[:, 1792:1920]
        bv_wide = raw[:, 1920:2048]
        mixing = raw[:, 2048:2176]
        diagonal = raw[:, 2176:2304]
        mixT_f = raw[:, 2304:2432]
        bk_wide = raw[:, 2432:2560]
        shift_rows = raw[:, 2560:2688]
        columns = raw[:, 2688:2704]
        bq_col, bk_col, bv_col, alpha_col, gamma_col = (columns[:, i:i + 1] for i in range(5))
        row_sum, parent, keep, row_const = (columns[:, i:i + 1] for i in range(5, 9))
        bih_rows = raw[0:16, 2816:2944]
        bhh_rows = raw[0:16, 2944:3072]

        N_CONST = 15
        (PE_TRANSPOSED, PE_FOLDED, PE_SHIFTS, PE_MIXT, PE_OUTBIAS) = range(1, 6)
        PE_BIAS = 6
        LSTM_JOBS = [("ih", 1), ("ih", 2), ("ih", 3), ("ih", 4), ("hh", 2), ("hh", 3), ("hh", 4)]
        GATE_PARTS = [(0, 2, 0.5), (2, 3, 1.0), (3, 4, 0.5)]
        DVE_WIDE = 4

        def lstm_scale(kind, p, s):
            return s if kind == "ih" and p == 1 else 0.5 * s

        def lstm_dst(kind, p, half_index):
            w, base = (wih, (p - 1) * 4) if kind == "ih" else (whh, (p - 2) * 4)
            return w[half_index][:, base * 128:(base + 4) * 128]

        DVE_AP = 9
        DVE_MIXT = 10
        DVE_SHIFT_ROWS = 11
        DVE_BIAS_ROWS = 12
        SETUP_DVE = 35
        FIRST_WEIGHTS = 3

        def weights_due(it, k):
            j = k - FIRST_WEIGHTS
            return [j] if isinstance(it, int) and it == -1 and 0 <= j < len(LSTM_JOBS) else []

        block = ctx.enter_context(nc.Block())

        def iterations(eng, body):
            for it in range(-1, LOOP_FIRST):
                body(it, it % 2)
            with eng.Fori(0, LOOP_ROUNDS) as pair:
                body(pair * 2 + LOOP_FIRST, LOOP_FIRST % 2)
                body(pair * 2 + (LOOP_FIRST + 1), (LOOP_FIRST + 1) % 2)
            for it in range(LOOP_FIRST + 2 * LOOP_ROUNDS, NG + 3):
                body(it, it % 2)

        x_quads = x.rearrange("(n b) t d -> n t b d", b=QB)
        out_quads = out.rearrange("(n b) t d -> n t b d", b=QB)

        @block.sync
        def _(sp):
            def load_const(dst, src):
                sp.dma_start(dst, src).then_inc(const_loaded, 16)

            with nc.allow_non_contiguous_dma(reason="bias columns, 4 bytes each"):
                load_const(raw_at["adj"], adj)
                for name, w in (("Wq", Wq), ("Wk", Wk), ("Wv", Wv), ("Wo", Wo), ("Wg0", Wg0), ("Wg1", Wg1)):
                    load_const(raw_at[name], w)
                for name, b in (("bg0", bg0), ("bg1", bg1), ("bo", bo)):
                    load_const(raw_at[name], b.rearrange("(a d) -> a d", a=1).to_broadcast([128, 128]))
                for col, b in ((bq_col, bq), (bk_col, bk), (bv_col, bv)):
                    load_const(col, b.rearrange("(d a) -> d a", a=1))
                for col, b in ((alpha_col, alpha), (gamma_col, gamma)):
                    load_const(col, b.rearrange("(a d) -> a d", a=1).to_broadcast([128, 1]))
                for q in range(NQ):
                    sp.dma_start(quad(xg[:, q * QW:(q + 1) * QW]), x_quads[q]).then_inc(xg_loaded[q], 16)
                sp.dma_start(raw_ih[:].rearrange("r (g h) -> r g h", g=16),
                             Wih.rearrange("p (g r) h -> r (p g) h", g=4)).then_inc(lstm_loaded, 16)
                sp.dma_start(raw_hh[:].rearrange("r (g h) -> r g h", g=16),
                             Whh.rearrange("p (g r) h -> r (p g) h", g=4)).then_inc(lstm_loaded, 16)
                sp.dma_start(bih_rows, bih.rearrange("p (g h) -> (p g) h", g=4)).then_inc(lstm_loaded, 16)
                sp.dma_start(bhh_rows, bhh.rearrange("p (g h) -> (p g) h", g=4)).then_inc(lstm_loaded, 16)

                for q in range(NQ):
                    sp.dma_start(quad(x1[:, q * QW:(q + 1) * QW]), x_quads[q]).then_inc(x1_loaded[q], 16)

            def body(it, parity):
                for k in range(NSTEP):
                    for place, wrap, part in due(SP_PARTS, it, k):
                        job = (it, parity, place, wrap)
                        stage, q, _ = entry(job)
                        g = group_of(job)
                        cols = slice(q * QW, (q + 1) * QW)
                        if not present(job):
                            continue
                        if stage == "AGG1":
                            if isinstance(g, int) and g == 0:
                                continue
                            wait(sp, x_split, nth(g - 1, q))
                            sp.dma_start(quad(xg[:, cols]), x_quads[g * NQ + q]).then_inc(xg_loaded[q], 16)
                        elif part == "load":
                            if not in_range(g + 1):
                                continue
                            bank_read(sp, job)
                            sp.dma_start(quad(x1[:, cols]), x_quads[(g + 1) * NQ + q]).then_inc(x1_loaded[q], 16)
                        else:
                            wait(sp, y2_ready, nth(g, q))
                            sp.dma_start(out_quads[g * NQ + q], quad(y2[q][:])).then_inc(y2_stored[q], 16)
            iterations(sp, body)
            for q in range(NQ):
                sp.wait_ge(y2_stored[q], 16 * NG)

        @block.gpsimd
        def _(pool):
            pool.memset(half[:], 0.5).then_inc(setup_pool, 1)
            pool.memset(one[:], 1.0).then_inc(setup_pool, 1)
            pool.memset(inv_d[:], 1.0 / D).then_inc(setup_pool, 1)
            pool.memset(eps[:], EPS).then_inc(setup_pool, 1)
            pool.memset(neg_half[:], -0.5).then_inc(setup_pool, 1)
            pool.memset(ident[:], 0.0).then_inc(setup_pool, 1)
            pool.wait_ge(setup_pool, 6)
            pool.affine_select(out=ident[:], in_=ident[:], compare_op=ALU.not_equal, fill=1.0,
                               base=0, pattern=[[-1, 128]], channel_multiplier=1).then_inc(setup_pool, 1)

            chain_length = 6
            norms = [0]

            def body(it, parity):
                if isinstance(it, int) and it == LOOP_FIRST + 2 * LOOP_ROUNDS:
                    norms[0] += (LOOP_ROUNDS - 1) * 2 * 2 * NQ

                def step(ins, n):
                    ins.then_inc(pool_step, 1)
                    done = norms[0] * chain_length + n
                    if not isinstance(it, int):
                        rate = 2 * NQ * chain_length
                        first = LOOP_FIRST + (parity != LOOP_FIRST % 2)
                        done = it * rate + (done - first * rate)
                    pool.wait_ge(pool_step, done)

                def normalise(stats, q, tile, ready):
                    st = stats[:, q * QB * 6:(q + 1) * QB * 6].rearrange("p (b s) -> p b s", s=6)
                    m = moments[:].rearrange("p (k b) -> p k b", b=QB)
                    pair = moments[:, 0:8].rearrange("p (k b) -> p b k", b=QB)
                    tt = pool.tensor_tensor
                    tt(m[:, 4], st[:, :, 2], st[:, :, 5], ALU.add)
                    step(tt(pair, st[:, :, 1:5:3], half[:].rearrange("p (b k) -> p b k", b=QB), ALU.mult), 1)
                    tt(m[:, 5], m[:, 4], inv_d[:], ALU.mult)
                    tt(m[:, 2], m[:, 0], m[:, 1], ALU.add)
                    step(tt(m[:, 3], m[:, 0], m[:, 1], ALU.subtract), 2)
                    tt(m[:, 4], m[:, 5], eps[:], ALU.add)
                    step(tt(m[:, 6], m[:, 3], m[:, 3], ALU.mult), 3)
                    step(tt(m[:, 7], m[:, 4], m[:, 6], ALU.add), 4)
                    step(tt(m[:, 6], m[:, 7], neg_half[:], ALU.pow), 5)
                    step(tt(quad(tile), quad(tile), m[:, 2].unsqueeze(2).to_broadcast([128, QB, 128]), ALU.subtract), 6)
                    tt(quad(tile), quad(tile), m[:, 6].unsqueeze(2).to_broadcast([128, QB, 128]),
                       ALU.mult).then_inc(ready, 1)
                    norms[0] += 1

                def split_x(job, q):
                    g = group_of(job)
                    n = q % 2
                    src = xg[:, q * QW:(q + 1) * QW]
                    wait(pool, xg_loaded[q], 16 * (g + 1))
                    before = find(job, "AGG1", (q - 2) % NQ, int(q < 2))
                    if before and present(before):
                        bank_read(pool, before)
                    pool.tensor_tensor(xs[n][0][:], src, one[:].to_broadcast([128, QW]), ALU.mult).then_inc(x_hi, 1)
                    wait(pool, x_hi, nth(g, q))
                    pool.tensor_tensor(xs[n][1][:], src, f32(xs[n][0][:]), ALU.subtract).then_inc(x_split, 1)

                for k in range(NSTEP):
                    for place, wrap, part in due(POOL_PARTS, it, k):
                        job = (it, parity, place, wrap)
                        stage, q, _ = entry(job)
                        g = group_of(job)
                        if not present(job):
                            continue
                        if stage == "AGG1":
                            split_x(job, q)
                        elif stage == "LN1":
                            wait(pool, y1_stats, nth(g, q))
                            normalise(stats1, q, x1[:, q * QW:(q + 1) * QW], x1_ready)
                        elif stage == "KQ":
                            if not draining(job):
                                prepare(pool, job)
                        elif stage == "SCORE":
                            wait(pool, exp_inverse, nth(g, q))
                            pool.tensor_tensor(quad(prob[:]), quad(expo[:]),
                                               exp_inv[:].unsqueeze(2).to_broadcast([128, QB, 128]),
                                               ALU.mult).then_inc(prob_ready, 1)
                        else:
                            wait(pool, y2_stats, nth(g, q))
                            normalise(stats2, q, y2[q][:], y2_ready)
            iterations(pool, body)

        @block.scalar
        def _(act):
            def copy(dst, src, **kw):
                return act.activation(dst, src, ACT.Copy, **kw)

            def split_weights(j):
                kind, p = LSTM_JOBS[j]
                act.wait_ge(weights_transposed, j + 1)
                for a, b, s in GATE_PARTS:
                    copy(lstm_dst(kind, p, 0)[:, a * 128:b * 128], gate_bank[j % 4][:, a * 128:b * 128],
                         scale=lstm_scale(kind, p, s)).then_inc(weights_hi, 1)

            def side_part(job, part):
                stage, q, _ = entry(job)
                bank = side_bank[turn(job)[0]][:]
                g = group_of(job)
                h2 = [tile[:, q * QW:(q + 1) * QW] for tile in state[parity_of(job)]]
                done = act_hi.get(stage)
                if stage in ("AGG1", "AGG2", "XT", "VAL", "PT"):
                    dst = {"AGG1": agg1, "AGG2": agg2, "XT": x1T[q % 2], "VAL": value[q % 2], "PT": probT}[stage]
                    products_done(act, job)
                    copy(dst[0][:], bank).then_inc(done, 1)
                elif stage == "KQ" and part == "shift":
                    wait(act, row_product_ready, nth(g, q))
                    for b in range(QB):
                        ins = copy(bat(row_product, b), bat(row_product, b),
                                   accum_out=row_shift[:, q * QB + b:q * QB + b + 1])
                    ins.then_inc(row_ready, 1)
                elif stage == "KQ":
                    products_done(act, job)
                    act.activation(query[0][:], bank, ACT.Identity, bias=key_bias[:, 0:1]).then_inc(done, 1)
                elif stage in ("PROJ1", "PROJ2"):
                    bank_read(act, job)
                    src, dst = (sum1[:], h1[0][:]) if stage == "PROJ1" else (sum2[:], h2[0])
                    act.activation(dst, src, ACT.Relu).then_inc(done, 1)
                elif part == "exp":
                    wait(act, score_max, nth(g, q))
                    for b in range(QB):
                        ins = act.activation(bat(expo, b), bat(score, b), ACT.Exp, bias=neg_max[:, b:b + 1],
                                             accum_out=exp_sum[:, b:b + 1])
                    ins.then_inc(exp_ready, 1)
                else:
                    bank_read(act, job)
                    copy(refined_parts[0][:], refined[:]).then_inc(done, 1)

            def side_parts(it, parity, k, when):
                for place, wrap, part in due(ACT_PARTS, it, k, when):
                    if present((it, parity, place, wrap)):
                        side_part((it, parity, place, wrap), part)

            def body(it, parity):
                for k, (p, c, s) in enumerate(STEPS):
                    if has_step(it, k):
                        for gate in (GI, GG, GF, GO):
                            if gate == GF and s == 0:
                                continue
                            wait(act, gate_ready[gate], gate_uses(it, gate, k) + 1)
                            act.activation(packed(gate_tile(it, k, gate), p), packed(gate_bank[gate], p), ACT.Tanh,
                                           bias=gate_bias[:, w_index(p, gate):w_index(p, gate) + 1]
                                           ).then_inc(gate_read[gate], 1)
                    side_parts(it, parity, k, EARLY)
                    if has_step(it, k):
                        wait(act, cell_ready, steps_before(it, k) + 1)
                        act.activation(packed(cell_tanh, p), cell_of(p, c), ACT.Tanh, scale=0.5
                                       ).then_inc(cell_tanh_ready, 1)
                    side_parts(it, parity, k, LATE)
                    for j in weights_due(it, k):
                        split_weights(j)
            iterations(act, body)

        @block.vector
        def _(dve):
            count = [0]

            def done(ins):
                count[0] += 1
                ins.then_inc(setup_dve, 1)

            def own():
                dve.wait_ge(setup_dve, count[0])

            ts, tt, stt, cp = dve.tensor_scalar, dve.tensor_tensor, dve.scalar_tensor_tensor, dve.tensor_copy
            dve.wait_ge(const_loaded, 16 * N_CONST)
            dve.wait_ge(setup_pe, PE_TRANSPOSED)
            done(cp(transposed, side_bank[0][:]))
            done(cp(bq_wide, bq_col.to_broadcast([128, 128])))
            done(cp(bv_wide, bv_col.to_broadcast([128, 128])))
            done(cp(bk_wide, bk_col.to_broadcast([128, 128])))
            assert count[0] == DVE_WIDE
            done(dve.reduce_sum(row_sum, raw_at["adj"], AX.X))
            own()
            done(ts(parent, row_sum, 0.0, gamma_col, ALU.is_gt, ALU.mult))
            own()
            done(ts(keep, parent, -1.0, 1.0, ALU.mult, ALU.add))
            own()
            dve.wait_ge(setup_pool, 7)
            done(ts(diagonal, ident[:], keep, None, ALU.mult))
            own()
            done(stt(out=mixing, in0=raw_at["adj"], scalar=parent, in1=diagonal, op0=ALU.mult, op1=ALU.add))
            assert count[0] == DVE_AP
            dve.wait_ge(setup_pe, PE_MIXT)
            done(cp(mixT_f, side_bank[3][:, 0:128]))
            assert count[0] == DVE_MIXT
            dve.wait_ge(setup_pe, PE_SHIFTS)
            done(tt(shift_rows, side_bank[2][:, 0:128], raw_at["bo"], ALU.add))
            assert count[0] == DVE_SHIFT_ROWS
            dve.wait_ge(lstm_loaded, 64)
            done(tt(bih_rows, bih_rows, bhh_rows, ALU.add))
            assert count[0] == DVE_BIAS_ROWS
            done(ts(key_bias[:], side_bank[2][:, 128:129], SCALE, None, ALU.mult))
            dve.wait_ge(setup_pe, PE_FOLDED)
            done(ts(query_row[:], side_bank[3][:, 128:256], SCALE, None, ALU.mult))
            done(ts(row_const, side_bank[2][:, 130:131], SCALE, None, ALU.mult))
            dve.wait_ge(setup_pe, PE_FOLDED)
            done(cp(bias1[:], side_bank[1][:, 0:128]))
            done(cp(bias2[:], side_bank[1][:, 128:256]))
            done(ts(kq[0][:], side_bank[1][:, 256:384], SCALE, None, ALU.mult))
            done(cp(vo[0][:], side_bank[1][:, 384:512]))
            own()
            done(cp(adjT[0][:], adjT_f))
            done(cp(wg0[0][:], raw_at["Wg0"]))
            done(cp(wg1[0][:], raw_at["Wg1"]))
            done(cp(mixT[0][:], mixT_f))
            done(ts(mask_bias[:], raw_at["adj"], 0.0, MASKED, ALU.is_equal, ALU.mult))
            own()
            done(stt(out=kq[1][:], in0=side_bank[1][:, 256:384], scalar=SCALE, in1=f32(kq[0][:]),
                     op0=ALU.mult, op1=ALU.subtract))
            done(tt(vo[1][:], side_bank[1][:, 384:512], f32(vo[0][:]), ALU.subtract))
            done(tt(adjT[1][:], adjT_f, f32(adjT[0][:]), ALU.subtract))
            done(tt(wg0[1][:], raw_at["Wg0"], f32(wg0[0][:]), ALU.subtract))
            done(tt(wg1[1][:], raw_at["Wg1"], f32(wg1[0][:]), ALU.subtract))
            done(tt(mixT[1][:], mixT_f, f32(mixT[0][:]), ALU.subtract))
            done(stt(out=mask_bias[:], in0=raw_at["adj"], scalar=alpha_col, in1=mask_bias[:],
                     op0=ALU.mult, op1=ALU.add))
            own()
            done(ts(mask_bias[:], mask_bias[:], row_const, None, ALU.add))
            dve.wait_ge(setup_pe, PE_OUTBIAS)
            done(cp(out_bias[:], gate_bank[0][:, 0:128]))
            dve.wait_ge(setup_pe, PE_BIAS)
            done(ts(gate_bias[:], gate_bank[1][:, 0:16], 0.5, None, ALU.mult))
            own()
            done(cp(gate_bias[:, 2:16:4], gate_bank[1][:, 2:16:4]))
            assert count[0] == SETUP_DVE, count[0]

            def split_weights(j):
                kind, p = LSTM_JOBS[j]
                dve.wait_ge(weights_hi, 3 * (j + 1))
                for a, b, s in GATE_PARTS:
                    cols = slice(a * 128, b * 128)
                    stt(out=lstm_dst(kind, p, 1)[:, cols], in0=gate_bank[j % 4][:, cols],
                        scalar=lstm_scale(kind, p, s), in1=f32(lstm_dst(kind, p, 0)[:, cols]),
                        op0=ALU.mult, op1=ALU.subtract).then_inc(weights_lo, 1)

            def side_part(job, part):
                stage, q, _ = entry(job)
                number, _ = turn(job)
                bank = side_bank[number][:]
                read = side_read[number]
                g = group_of(job)
                h2 = [tile[:, q * QW:(q + 1) * QW] for tile in state[parity_of(job)]]
                if stage in ("AGG1", "AGG2", "XT", "VAL", "PT"):
                    dst = {"AGG1": agg1, "AGG2": agg2, "XT": x1T[q % 2], "VAL": value[q % 2], "PT": probT}[stage]
                    wait(dve, act_hi[stage], nth(g, q))
                    tt(dst[1][:], bank, f32(dst[0][:]), ALU.subtract).then_inc(read, 1)
                elif stage == "KQ" and part == "prepare":
                    if draining(job):
                        prepare(dve, job)
                elif stage == "KQ":
                    wait(dve, act_hi[stage], nth(g, q))
                    stt(out=query[1][:], in0=bank, scalar=key_bias[:, 0:1], in1=f32(query[0][:]),
                        op0=ALU.add, op1=ALU.subtract).then_inc(read, 1)
                elif stage in ("PROJ1", "PROJ2"):
                    total, const = (sum1, bias1) if stage == "PROJ1" else (sum2, bias2)
                    if part == "sum":
                        products_done(dve, job)
                        tt(quad(total[:]), quad(bank), spread(const[:]), ALU.add).then_inc(read, 1)
                    else:
                        hi, lo = ((h1[0][:], h1[1][:]) if stage == "PROJ1"
                                  else (h2[0], h2[1]))
                        wait(dve, act_hi[stage], nth(g, q))
                        stt(out=lo, in0=total[:], scalar=0.0, in1=f32(hi), op0=ALU.max, op1=ALU.subtract
                            ).then_inc(h1_split if stage == "PROJ1" else h2_split, 1)
                elif stage == "LN1":
                    dst = x1[:, q * QW:(q + 1) * QW]
                    wait(dve, x1_loaded[q], 16 * (g + 1))
                    products_done(dve, job)
                    stt(out=dst, in0=bank, scalar=0.5, in1=dst, op0=ALU.mult, op1=ALU.add).then_inc(read, 1)
                    bank_read(dve, job)
                    for b in range(QB):
                        ins = dve.bn_stats(quad_stats(stats1, q, b), bat(dst, b))
                    ins.then_inc(y1_stats, 1)
                elif stage == "SCORE" and part == "sum":
                    products_done(dve, job)
                    wait(dve, row_ready, nth(g, q))
                    for b in range(QB):
                        ins = stt(out=bat(score, b), in0=bat(bank, b), scalar=row_shift[:, q * QB + b:q * QB + b + 1],
                                  in1=mask_bias[:], op0=ALU.add, op1=ALU.add)
                    ins.then_inc(read, 1)
                    bank_read(dve, job)
                    dve.tensor_reduce(neg_max[:], quad(score[:]), AX.X, ALU.max, negate=True).then_inc(score_max, 1)
                elif stage == "SCORE" and part == "inv":
                    wait(dve, exp_ready, nth(g, q))
                    dve.reciprocal(exp_inv[:], exp_sum[:]).then_inc(exp_inverse, 1)
                elif stage == "PV" and part == "sum":
                    products_done(dve, job)
                    tt(refined[:], bank, x1[:, q * QW:(q + 1) * QW], ALU.add).then_inc(read, 1)
                elif stage == "PV":
                    wait(dve, act_hi[stage], nth(g, q))
                    tt(refined_parts[1][:], refined[:], f32(refined_parts[0][:]), ALU.subtract
                       ).then_inc(refined_split, 1)
                else:
                    dst = y2[q]
                    products_done(dve, job)
                    wait(dve, y2_base, nth(g, q))
                    tt(dst[:], bank, dst[:], ALU.add).then_inc(read, 1)
                    bank_read(dve, job)
                    for b in range(QB):
                        ins = dve.bn_stats(quad_stats(stats2, q, b), bat(dst, b))
                    ins.then_inc(y2_stats, 1)

            def new_cell(it, k):
                p, c, s = STEPS[k]
                ti, tf, tg = (packed(gate_tile(it, k, g), p) for g in (GI, GF, GG))
                old = cell_of(p, c)
                before = steps_before(it, k, lambda step: step[2] > 0) * 2
                wait(dve, gate_read[GG], gate_uses(it, GG, k) + 1)
                if s == 0:
                    stt(out=old, in0=ti, scalar=1.0, in1=tg, op0=ALU.add, op1=ALU.mult).then_inc(cell_ready, 1)
                    return
                stt(out=ti, in0=ti, scalar=1.0, in1=tg, op0=ALU.add, op1=ALU.mult).then_inc(cell_term, 1)
                wait(dve, gate_read[GF], gate_uses(it, GF, k) + 1)
                stt(out=tf, in0=tf, scalar=1.0, in1=old, op0=ALU.add, op1=ALU.mult).then_inc(cell_term, 1)
                wait(dve, cell_term, before + 2)
                stt(out=old, in0=tf, scalar=0.5, in1=ti, op0=ALU.mult, op1=ALU.add).then_inc(cell_ready, 1)

            def new_hidden(it, k, parity):
                p, c, s = STEPS[k]
                to = packed(gate_tile(it, k, GO), p)
                parity = (parity - (p == 4)) % 2
                kept = s == p - 1
                full = window(final[parity], p, c, s) if kept else packed(fresh, p)
                count = steps_before(it, k) + 1
                wait(dve, gate_read[GO], gate_uses(it, GO, k) + 1)
                wait(dve, cell_tanh_ready, count)
                stt(out=full, in0=to, scalar=1.0, in1=packed(cell_tanh, p), op0=ALU.add, op1=ALU.mult
                    ).then_inc(h_full, 1)
                if not is_split((p, c, s)):
                    return
                hi, lo = ((window(t, p, c, s) for t in state[parity]) if kept
                          else (packed(t, p) for t in hidden[lane(p, c)]))
                wait(dve, h_full, count)
                cp(hi, full).then_inc(h_hi, 1)
                wait(dve, h_hi, splits_before(it, k) + 1)
                tt(lo, full, f32(hi), ALU.subtract).then_inc(h_split, 1)

            def side_parts(it, parity, k, when):
                for place, wrap, part in due(DVE_PARTS, it, k, when):
                    if present((it, parity, place, wrap)):
                        side_part((it, parity, place, wrap), part)

            def body(it, parity):
                for k in range(NSTEP):
                    if has_step(it, k):
                        new_cell(it, k)
                    side_parts(it, parity, k, EARLY)
                    if has_step(it, k):
                        new_hidden(it, k, parity)
                    side_parts(it, parity, k, LATE)
                    for j in weights_due(it, k):
                        split_weights(j)
            iterations(dve, body)

        @block.tensor
        def _(pe):
            def mm(dst, lhsT, rhs, start, stop):
                return nc.tensor.matmul(dst, lhsT, rhs, start=start, stop=stop)

            pe.wait_ge(const_loaded, 16 * N_CONST)
            pe.wait_ge(setup_pool, 7)
            for i, name in enumerate(("adj", "Wq", "Wk", "Wv")):
                ins = nc.tensor.transpose(bat(side_bank[0], i), raw_at[name], ident[:])
            ins.then_inc(setup_pe, 1)
            pe.wait_ge(setup_dve, DVE_WIDE)
            mm(side_bank[3][:, 128:256], bk_wide, wqT, True, True)
            mm(side_bank[1][:, 0:128], adjT_f, raw_at["bg0"], True, True)
            mm(side_bank[1][:, 128:256], raw_at["bg1"], adjT_f, True, True)
            mm(side_bank[1][:, 256:384], wqT, wkT, True, True)
            mm(side_bank[1][:, 384:512], wvT, raw_at["Wo"], True, True).then_inc(setup_pe, 1)
            mm(side_bank[2][:, 0:128], bv_wide, raw_at["Wo"], True, True)
            mm(side_bank[2][:, 128:129], wkT, bq_col, True, True)
            mm(side_bank[2][:, 130:131], bq_wide, bk_col, True, True).then_inc(setup_pe, 1)
            pe.wait_ge(setup_dve, DVE_AP)
            nc.tensor.transpose(side_bank[3][:, 0:128], mixing, ident[:]).then_inc(setup_pe, 1)
            pe.wait_ge(setup_dve, DVE_SHIFT_ROWS)
            mm(gate_bank[0][:, 0:128], mixT_f, shift_rows, True, True).then_inc(setup_pe, 1)
            pe.wait_ge(setup_dve, DVE_BIAS_ROWS)
            nc.tensor.transpose(gate_bank[1][:, 0:16], bih_rows, ident[0:16, 0:16]).then_inc(setup_pe, 1)
            pe.wait_ge(setup_dve, SETUP_DVE)

            def transpose_weights(j):
                kind, p = LSTM_JOBS[j]
                if j >= 4:
                    pe.wait_ge(weights_lo, 3 * (j - 3))
                src = raw_ih if kind == "ih" else raw_hh
                for gate in range(4):
                    ins = nc.tensor.transpose(bat(gate_bank[j % 4], gate), bat(src, w_index(p, gate)), ident[:])
                ins.then_inc(weights_transposed, 1)

            def three(dst, a, b, start, stop):
                mm(dst, a[0], b[0], start, False)
                mm(dst, a[0], b[1], False, False)
                return mm(dst, a[1], b[0], False, stop)

            def both(pair, cut):
                return [cut(t) for t in pair]

            def side_job(job):
                stage, q, _ = entry(job)
                number, before = turn(job)
                bank = side_bank[number]
                g = group_of(job)
                wait(pe, side_read[number], before)

                def per_batch(a, b_of):
                    for i in range(QB):
                        ins = three(bat(bank, i), both(a, lambda t: bat(t, i)), b_of(i), True, True)
                    return ins

                if stage == "AGG1":
                    wait(pe, x_split, nth(g, q))
                    ins = per_batch(xs[q % 2], lambda i: both(adjT, lambda t: t[:]))
                elif stage == "PROJ1":
                    bank_read(pe, find(job, "AGG1", q))
                    ins = per_batch(agg1, lambda i: both(wg0, lambda t: t[:]))
                elif stage == "AGG2":
                    wait(pe, h1_split, nth(g, q))
                    ins = per_batch(h1, lambda i: both(adjT, lambda t: t[:]))
                elif stage == "PROJ2":
                    bank_read(pe, find(job, "AGG2", q))
                    ins = three(bank[:], both(wg1, lambda t: t[:]), both(agg2, lambda t: t[:]), True, True)
                elif stage == "LN1":
                    wait(pe, h_full, steps_before(g + 1, STEPS.index((4, 0, 3))) + 1)
                    for i in range(QB):
                        ins = nc.tensor.transpose(bat(bank, i), bat(final[parity_of(job)], q * QB + i), ident[:])
                elif stage == "XT":
                    wait(pe, x1_ready, nth(g, q))
                    for i in range(QB):
                        ins = nc.tensor.transpose(bat(bank, i), bat(x1, q * QB + i), ident[:])
                elif stage == "KQ":
                    bank_read(pe, find(job, "XT", q))
                    ins = three(bank[:], both(kq, lambda t: t[:]), both(x1T[q % 2], lambda t: t[:]), True, True)
                elif stage == "VAL":
                    ins = per_batch(x1T[q % 2], lambda i: both(vo, lambda t: t[:]))
                elif stage == "SCORE":
                    bank_read(pe, find(job, "KQ", q))
                    ins = per_batch(query, lambda i: both(x1T[q % 2], lambda t: bat(t, i)))
                elif stage == "PT":
                    wait(pe, prob_ready, nth(g, q))
                    for i in range(QB):
                        ins = nc.tensor.transpose(bat(bank, i), bat(prob, i), ident[:])
                elif stage == "PV":
                    needed = {turn(ref)[0]: ref for ref in sorted(
                        (find(job, "PT", q), find(job, "VAL", q)), key=lambda ref: (-ref[3], ref[2]))}
                    for at, ref in needed.items():
                        if at != number:
                            bank_read(pe, ref)
                    ins = per_batch(probT, lambda i: both(value[q % 2], lambda t: bat(t, i)))
                else:
                    wait(pe, refined_split, nth(g, q))
                    ins = three(bank[:], both(mixT, lambda t: t[:]), both(refined_parts, lambda t: t[:]), True, True)
                ins.then_inc(side_ready[number], 1)

            def lstm_step(it, k, parity):
                p, c, s = STEPS[k]
                used = [g for g in (GI, GG, GF, GO) if g != GF or s > 0]
                own_state = state[(parity - (p == 4)) % 2]
                if p == 1:
                    wait(pe, h2_split, nth(it, c))
                elif p == 4:
                    wait(pe, h_split, splits_before(it, 0))
                else:
                    end = (1, 2 * c + 1, 0) if p == 2 else (2, c, 1)
                    wait(pe, h_split, splits_before(it, STEPS.index(end)) + 1)
                inputs = both(own_state, lambda t: window(t, p, c, s))
                for gate in used:
                    at = w_index(p, gate)
                    wait(pe, gate_read[gate], gate_uses(it, gate, k))
                    ins = three(packed(gate_bank[gate], p), both(wih, lambda t: bat(t, at)), inputs, True, s == 0)
                    if s == 0:
                        ins.then_inc(gate_ready[gate], 1)
                if s > 0:
                    wait(pe, h_split, splits_before(it, STEPS.index((p, c, s - 1))) + 1)
                    for gate in used:
                        at = (p - 2) * 4 + gate
                        three(packed(gate_bank[gate], p), both(whh, lambda t: bat(t, at)),
                              both(hidden[lane(p, c)], lambda t: packed(t, p)), False, True
                              ).then_inc(gate_ready[gate], 1)

            def body(it, parity):
                for k in range(NSTEP):
                    if has_step(it, k):
                        lstm_step(it, k, parity)
                    slots = fill(it if isinstance(it, int) else None)
                    first = sum(len(slot) for slot in slots[:k])
                    for place in range(first, first + len(slots[k])):
                        if present((it, parity, place, 0)):
                            side_job((it, parity, place, 0))
                    for j in weights_due(it, k):
                        transpose_weights(j)
                if isinstance(it, int) and it == -1:
                    pe.wait_ge(weights_lo, 3 * len(LSTM_JOBS))
            iterations(pe, body)


_INS = ['x', 'adj', 'L0_gnn_Wg0', 'L0_gnn_bg0', 'L0_gnn_Wg1', 'L0_gnn_bg1', 'L0_gnn_Wih', 'L0_gnn_Whh',
        'L0_gnn_bih', 'L0_gnn_bhh', 'L1_gnn_Wq', 'L1_gnn_bq', 'L1_gnn_Wk', 'L1_gnn_bk', 'L1_gnn_Wv',
        'L1_gnn_bv', 'L1_gnn_Wo', 'L1_gnn_bo', 'L1_gnn_alpha', 'L1_gnn_gamma']


def kernel(**inputs):
    import numpy as _np
    import concourse.bacc as _bacc
    from concourse import mybir as _mybir
    from concourse.bass_utils import run_bass_kernel_spmd as _run

    nc = _bacc.Bacc("TRN2", target_bir_lowering=False, num_devices=1)
    arrays, args = {}, []
    for name in _INS:
        a = _np.ascontiguousarray(inputs[name]).reshape(_np.shape(inputs[name]) or (1,))
        arrays[f"in_{name}_dram"] = a
        args.append(nc.dram_tensor(f"in_{name}_dram", a.shape, _mybir.dt.from_np(a.dtype), kind="ExternalInput").ap())
    args.append(nc.dram_tensor("out_0_dram", (NB, T, D), F32, kind="ExternalOutput").ap())
    graph_resnorm_kernel(nc, *args)
    r = _run(nc, [arrays], core_ids=[0])
    return r.results[0]["out_0_dram"]
```
